# Optimizing a Trainium2 kernel written in Bass

```python
import numpy as np
import jax
import jax.numpy as jnp

def _softmax(x, axis=-1):
    return jax.nn.softmax(x, axis=axis)

def _gelu(x):
    return jax.nn.gelu(x, approximate=True)

def _silu(x):
    return jax.nn.silu(x)

def _sigmoid(x):
    return jax.nn.sigmoid(x)

def _layernorm(x, axis=-1, eps=1e-05):
    m = jnp.mean(x, axis=axis, keepdims=True)
    v = jnp.var(x, axis=axis, keepdims=True)
    return (x - m) / jnp.sqrt(v + eps)

def _scatter_add(tgt, idx, src, axis=0):
    return tgt.at[idx].add(src)

def _segment_sum(src, seg, n):
    return jax.ops.segment_sum(src, seg, n)
kernel_name = 'mk_gnn_preln_d2_gnn_r8_d94118'

def setup_inputs(seed: int=0):
    np.random.seed(seed)
    _w = jnp.asarray

    def _rec_inputs():
        import jax
        import jax.numpy as jnp
        _gk = jax.random.key(seed)
        x = -0.000202 + 1 * jax.random.normal(jax.random.fold_in(_gk, 1), (12500, 128), jnp.float32)
        src = jax.random.randint(jax.random.fold_in(_gk, 2), (200000,), 0, 12500, jnp.int32)
        dst = jax.random.randint(jax.random.fold_in(_gk, 3), (200000,), 0, 12500, jnp.int32)
        _o = jnp.argsort(dst, stable=True)
        src = src[_o]
        dst = dst[_o]
        edge_attr_128 = -5.16925e-05 + 1.00005 * jax.random.normal(jax.random.fold_in(_gk, 11), (200000, 128), jnp.float32)
        return (x, src, dst, edge_attr_128)
    x, src, dst, edge_attr_128 = _rec_inputs()

    def _L0_gnn_setup():
        import jax, jax.numpy as jnp
        import numpy as np
        N_NODES = 6250
        N_EDGES = 100000
        D_IN = 128
        D_HID = 512
        D_OUT = 128
        key = jax.random.key(seed)
        k1, k2, k3, k4, k5, k6 = jax.random.split(key, 6)
        input_matrix = jax.random.normal(k1, (N_NODES, D_IN), dtype=jnp.float32)
        adjacency_coo_matrix = jax.random.randint(k2, (2, N_EDGES), 0, N_NODES, dtype=jnp.int64)
        lim_fc = 1.0 / np.sqrt(D_IN)
        fc_w = jax.random.uniform(k3, (D_IN, D_HID), dtype=jnp.float32, minval=-lim_fc, maxval=lim_fc)
        fc_b = jax.random.uniform(k4, (D_HID,), dtype=jnp.float32, minval=-lim_fc, maxval=lim_fc)
        lim_w = np.sqrt(6.0 / (D_IN + D_HID + D_OUT))
        weights_matrix = jax.random.uniform(k5, (D_IN + D_HID, D_OUT), dtype=jnp.float32, minval=-lim_w, maxval=lim_w)
        return {'input_matrix': input_matrix, 'fc_w': fc_w, 'fc_b': fc_b, 'weights_matrix': weights_matrix, 'adjacency_coo_matrix': adjacency_coo_matrix}
    _L0_gnn_all = _L0_gnn_setup()
    _L0_gnn_in = {k: v for k, v in _L0_gnn_all.items() if k in ('fc_w', 'fc_b', 'weights_matrix')}
    del _L0_gnn_all

    def _L1_gnn_setup():
        import jax, jax.numpy as jnp
        import numpy as np
        N, E, D = (6250, 100000, 128)
        LN_EPS = 1e-05
        key = jax.random.key(seed)
        ks = jax.random.split(key, 8)
        x = jax.random.normal(ks[0], (N, D), dtype=jnp.float32)
        edge_index = jax.random.randint(ks[1], (2, E), 0, N, dtype=jnp.int64)
        edge_attr = jax.random.normal(ks[2], (E, D), dtype=jnp.float32)
        s_msg = 1.0 / np.sqrt(2 * D)
        s_upd = 1.0 / np.sqrt(2 * D)
        W_msg = jax.random.uniform(ks[3], (2 * D, D), jnp.float32, -s_msg, s_msg)
        b_msg = jax.random.uniform(ks[4], (D,), jnp.float32, -s_msg, s_msg)
        W_upd = jax.random.uniform(ks[5], (2 * D, D), jnp.float32, -s_upd, s_upd)
        b_upd = jax.random.uniform(ks[6], (D,), jnp.float32, -s_upd, s_upd)
        gamma = jnp.ones((D,), jnp.float32)
        beta = jnp.zeros((D,), jnp.float32)
        return {'x': x, 'edge_index': edge_index, 'edge_attr': edge_attr, 'W_msg': W_msg, 'b_msg': b_msg, 'W_upd': W_upd, 'b_upd': b_upd, 'gamma': gamma, 'beta': beta}
    _L1_gnn_all = _L1_gnn_setup()
    _L1_gnn_in = {k: v for k, v in _L1_gnn_all.items() if k in ('W_msg', 'b_msg', 'W_upd', 'b_upd', 'gamma', 'beta')}
    del _L1_gnn_all
    return {'x': x, 'src': src, 'dst': dst, 'edge_attr_128': edge_attr_128, 'L0_gnn_fc_w': _L0_gnn_in['fc_w'], 'L0_gnn_fc_b': _L0_gnn_in['fc_b'], 'L0_gnn_weights_matrix': _L0_gnn_in['weights_matrix'], 'L1_gnn_W_msg': _L1_gnn_in['W_msg'], 'L1_gnn_b_msg': _L1_gnn_in['b_msg'], 'L1_gnn_W_upd': _L1_gnn_in['W_upd'], 'L1_gnn_b_upd': _L1_gnn_in['b_upd'], 'L1_gnn_gamma': _L1_gnn_in['gamma'], 'L1_gnn_beta': _L1_gnn_in['beta']}

def reference(x, src, dst, edge_attr_128, L0_gnn_fc_w, L0_gnn_fc_b, L0_gnn_weights_matrix, L1_gnn_W_msg, L1_gnn_b_msg, L1_gnn_W_upd, L1_gnn_b_upd, L1_gnn_gamma, L1_gnn_beta):
    import jax
    import jax.numpy as jnp

    def _L0_gnn_ref(input_matrix, fc_w, fc_b, weights_matrix, adjacency_coo_matrix):
        import jax, jax.numpy as jnp
        import numpy as np
        N_NODES = 6250
        N_EDGES = 100000
        D_IN = 128
        D_HID = 512
        D_OUT = 128
        edge_src, edge_trg = (adjacency_coo_matrix[0], adjacency_coo_matrix[1])
        n_nodes = input_matrix.shape[0]
        neighbors = input_matrix[edge_trg]
        neighbors_repr = jax.nn.relu(neighbors @ fc_w + fc_b)
        agg = jax.ops.segment_max(neighbors_repr, edge_src, num_segments=n_nodes)
        agg = jnp.maximum(agg, 0.0)
        concat = jnp.concatenate([input_matrix, agg], axis=1)
        return concat @ weights_matrix

    def _L1_gnn_ref(x, edge_index, edge_attr, W_msg, b_msg, W_upd, b_upd, gamma, beta):
        import jax, jax.numpy as jnp
        import numpy as np
        N, E, D = (6250, 100000, 128)
        LN_EPS = 1e-05
        src, dst = (edge_index[0], edge_index[1])
        n = x.shape[0]
        msg_in = jnp.concatenate([x[src], edge_attr], axis=-1)
        msg = jax.nn.relu(msg_in @ W_msg + b_msg)
        summed = jax.ops.segment_sum(msg, dst, num_segments=n)
        counts = jax.ops.segment_sum(jnp.ones((msg.shape[0],), x.dtype), dst, num_segments=n)
        mean_msg = summed / jnp.maximum(counts, 1.0)[:, None]
        h = jnp.concatenate([x, mean_msg], axis=-1) @ W_upd + b_upd
        mu = jnp.mean(h, axis=-1, keepdims=True)
        var = jnp.mean(jnp.square(h - mu), axis=-1, keepdims=True)
        h = (h - mu) * jax.lax.rsqrt(var + LN_EPS) * gamma + beta
        return jax.nn.relu(h + x)
    edge_index = jnp.stack([src, dst])
    h = jnp.maximum(_layernorm(x, axis=-1), 0.0)
    x = x + _L0_gnn_ref(h, L0_gnn_fc_w, L0_gnn_fc_b, L0_gnn_weights_matrix, edge_index)
    h = jnp.maximum(_layernorm(x, axis=-1), 0.0)
    x = x + _L1_gnn_ref(h, edge_index, edge_attr_128, L1_gnn_W_msg, L1_gnn_b_msg, L1_gnn_W_upd, L1_gnn_b_upd, L1_gnn_gamma, L1_gnn_beta)
    return x

_drawn_inputs = setup_inputs


def setup_inputs(seed=0):
    import zlib

    import numpy as np

    out = dict(_drawn_inputs(seed))
    spreads = {'L1_gnn_gamma': (1.0, 0.2), 'L1_gnn_beta': (0.0, 0.1)}
    factors = {'L1_gnn_b_msg': 5.351}
    for name, (base, spread) in spreads.items():
        noise = np.random.default_rng([zlib.crc32(name.encode()), seed]).standard_normal(out[name].shape)
        drawn = base * np.exp(spread * noise) if base else spread * noise
        out[name] = jnp.asarray(drawn.astype(out[name].dtype))
    for name, factor in factors.items():
        out[name] = (out[name] * factor).astype(out[name].dtype)
    return out
```

```python
from contextlib import ExitStack, contextmanager

import concourse.bass as bass
from concourse import mybir

ALU = mybir.AluOpType
ACT = mybir.ActivationFunctionType
F32 = mybir.dt.float32
BF16 = mybir.dt.bfloat16
I32 = mybir.dt.int32

P = 128
ROW = 2048
GROUP = 512
CH = ROW // GROUP
J = GROUP // P
NODE_BITS = 14
PAD = (1 << NODE_BITS) - 1
ONE_BIT = 1 << 30
RESET = -1e30
EPS = 1e-5
BATCH = 7
UNROLL = 2


class Shapes:
    def __init__(self, nodes, edges, d, hid):
        self.nodes, self.edges, self.d, self.hid = nodes, edges, d, hid
        self.tiles = -(-nodes // P)
        self.rows = -(-edges // ROW)
        self.full_rows = edges // ROW
        self.groups = -(-edges // GROUP)
        self.chunks = hid // P
        assert d == P and self.tiles % BATCH == 0 and nodes < PAD and self.rows <= P
        assert self.chunks == 4 and self.tiles == self.rows


def reach(eng, semaphore, value):
    if not isinstance(value, int) or value > 0:
        eng.wait_ge(semaphore, value)


@contextmanager
def phase(nc):
    used = []

    def semaphore(name):
        used.append(nc.alloc_semaphore(name))
        return used[-1]

    with ExitStack() as ctx:
        yield ctx, semaphore
    nc.clear_and_free_semaphores(used)
    nc.all_engine_barrier()


class Memory:
    pass


def setup(nc, s, mem, src, dst):
    with phase(nc) as (ctx, semaphore):
        padded = semaphore("padded")
        zeroed = semaphore("zeroed")
        iotas_done = semaphore("iotas_done")
        src_landed = semaphore("src_landed")
        dst_landed = semaphore("dst_landed")
        x_landed = semaphore("x_landed")
        weights_landed = semaphore("weights_landed")
        block = ctx.enter_context(nc.Block())
        full, rest = s.full_rows, s.edges - s.full_rows * ROW
        whole, rest_nodes = s.nodes // P, s.nodes % P
        assert rest and rest_nodes

        @block.gpsimd
        def _(pool):
            pool.memset(mem.ident_wide[:], 0.0).then_inc(zeroed, 1)
            pool.wait_ge(zeroed, 1)
            pool.affine_select(out=mem.ident_wide[:, 1:1 + P], in_=mem.ident_wide[:, 1:1 + P],
                               compare_op=ALU.not_equal, fill=1.0, base=0, pattern=[[-1, P]],
                               channel_multiplier=1).then_inc(iotas_done, 1)
            pool.iota(mem.node_number[:], [[P, s.tiles]], base=0, channel_multiplier=1,
                      allow_small_or_imprecise_dtypes=True).then_inc(iotas_done, 1)
            pool.iota(mem.row_number[:], [[1, P]], base=0, channel_multiplier=0).then_inc(iotas_done, 1)
            pool.iota(mem.partition_number[:], [[0, 1]], base=0, channel_multiplier=1).then_inc(iotas_done, 1)

        @block.vector
        def _(dve):
            dve.memset(mem.src_rows[:], PAD).then_inc(padded, 1)
            dve.memset(mem.dst_rows[:], PAD).then_inc(padded, 1)
            dve.memset(mem.x[:, whole * s.d:], 0.0).then_inc(padded, 1)
            dve.memset(mem.eps[:], EPS)
            dve.memset(mem.ones[:], 1.0)
            for n in range(2):
                dve.memset(mem.ends[n][:, 0:1], 0.0)
            dve.wait_ge(src_landed, 32)
            dve.tensor_copy(mem.src_given[:], mem.src_rows[:])
            dve.wait_ge(dst_landed, 32)
            dve.tensor_copy(mem.dst_given[:], mem.dst_rows[:])
            dve.wait_ge(iotas_done, 2)
            dve.tensor_scalar(mem.node_half[:], mem.node_number[:], 0.5, None, ALU.add)
            dve.tensor_copy(mem.ident_bf[:], mem.ident_wide[:, 1:1 + P])

        @block.scalar
        def _(act):
            for tile, array in mem.weights:
                act.dma_start(tile, array).then_inc(weights_landed, 16)
            act.wait_ge(weights_landed, 16 * len(mem.weights))

        @block.sync
        def _(sp):
            sp.wait_ge(padded, 3)
            for edge_end, rows, landed in ((src, mem.src_rows, src_landed), (dst, mem.dst_rows, dst_landed)):
                sp.dma_start(rows[0:full, :], edge_end[0:full * ROW].rearrange("(r c) -> r c", c=ROW)
                             ).then_inc(landed, 16)
                sp.dma_start(rows[full:full + 1, 0:rest],
                             edge_end[full * ROW:s.edges].rearrange("(r c) -> r c", r=1)).then_inc(landed, 16)
            sp.dma_start(mem.x[:, 0:whole * s.d].rearrange("p (t d) -> p t d", d=s.d),
                         mem.x_dram[0:whole * P, :].rearrange("(t p) d -> p t d", p=P)).then_inc(x_landed, 16)
            sp.dma_start(mem.x[0:rest_nodes, whole * s.d:], mem.x_dram[whole * P:s.nodes, :]
                         ).then_inc(x_landed, 16)
            sp.wait_ge(src_landed, 32)
            sp.wait_ge(dst_landed, 32)
            sp.wait_ge(x_landed, 32)




def make_tables(nc, s, mem, n, by_segment, gathered, index, resets, kind):
    R = s.rows
    heads_n = R * CH
    with phase(nc) as (ctx, semaphore):
        def sem(name):
            return semaphore(f"t{n}_{name}")

        column_turned, resets_made, heads_spread, diagonal_made, shifted, rows_stored, compared = (
            sem(x) for x in ("column_turned", "resets_made", "heads_spread", "diagonal_made", "shifted",
                             "rows_stored", "compared"))
        differs = ctx.enter_context(nc.sbuf_tensor(f"t{n}_differs", [P, ROW], F32))
        diagonal = ctx.enter_context(nc.sbuf_tensor(f"t{n}_diagonal", [R, R, CH], F32))
        turned = [ctx.enter_context(nc.psum_tensor(f"t{n}_turned{k}", [P, J, P], F32)) for k in range(CH)]
        head_bank = ctx.enter_context(nc.psum_tensor(f"t{n}_head_bank", [P, 512], F32))
        shift_bank = ctx.enter_context(nc.psum_tensor(f"t{n}_shift_bank", [P, 512], F32))
        block = ctx.enter_context(nc.Block())
        from_row_above = mem.ident_wide[:, 0:P]

        @block.tensor
        def _(pe):
            pe.matmul(shift_bank[:, 0:1], from_row_above, by_segment[:, ROW - 1:ROW],
                      start=True, stop=True).then_inc(shifted, 1)
            for ch in range(CH):
                for j in range(J):
                    c = ch * GROUP + j
                    turn = pe.transpose(turned[ch][:, j, 0:R], gathered[0:R, c:c + GROUP - J + 1:J],
                                        mem.ident[0:R, 0:R])
                turn.then_inc(column_turned, 1)
            pe.wait_ge(diagonal_made, 1)
            pe.matmul(head_bank[:, 0:heads_n], mem.ones[0:R, :], diagonal[:].rearrange("k r c -> k (r c)"),
                      start=True, stop=True).then_inc(heads_spread, 1)

        @block.vector
        def _(dve):
            first = by_segment[0:R, :].rearrange("r (c g) -> r c g", g=GROUP)[:, :, 0]
            dve.tensor_tensor(diagonal[:], mem.ident[0:R, 0:R].unsqueeze(2).to_broadcast([R, R, CH]),
                              first.unsqueeze(1).to_broadcast([R, R, CH]), ALU.mult).then_inc(diagonal_made, 1)
            dve.wait_ge(shifted, 1)
            to, op = (resets, ALU.is_equal) if kind == "keep" else (differs, ALU.not_equal)
            dve.tensor_tensor(to[:, 1:ROW], by_segment[:, 1:ROW], by_segment[:, 0:ROW - 1], op
                              ).then_inc(compared, 1)
            dve.tensor_tensor(to[:, 0:1], by_segment[:, 0:1], shift_bank[:, 0:1], op).then_inc(compared, 1)
            for ch in range(CH):
                dve.wait_ge(column_turned, ch + 1)
                to = index[:].rearrange("p (r c j) -> p c j r", c=CH, j=J)[:, ch, :, 0:R]
                dve.tensor_scalar(to, turned[ch][:, :, 0:R], float(s.tiles * P - 1), None, ALU.min)
            dve.wait_ge(heads_spread, 1)
            dve.tensor_copy(mem.heads[n][:], head_bank[:, 0:heads_n])
            if kind != "keep":
                dve.wait_ge(compared, 2)
                dve.tensor_scalar(resets[:], differs[:], RESET, None, ALU.mult).then_inc(resets_made, 1)

        @block.sync
        def _(sp):
            sp.dma_start(mem.segment_dram[n].rearrange("(r c) g -> r (c g)", c=CH), by_segment[0:R, :]
                         ).then_inc(rows_stored, 16)
            sp.wait_ge(rows_stored, 16)
            if kind != "keep":
                sp.wait_ge(resets_made, 1)
                sp.dma_start(mem.reset_dram.rearrange("(r c) g -> r (c g)", c=CH), resets[0:R, :]
                             ).then_inc(rows_stored, 16)
                sp.wait_ge(rows_stored, 32)


def unpack_sorted_keys(nc, s, mem):
    with phase(nc) as (ctx, semaphore):
        unpacked = semaphore("unpacked")
        field = [ctx.enter_context(nc.sbuf_tensor(f"field{n}", [P, ROW], I32)) for n in range(2)]
        block = ctx.enter_context(nc.Block())

        @block.vector
        def _(dve):
            bits = mem.sorted_keys[:].bitcast(I32)
            dve.tensor_scalar(field[0][:], bits, NODE_BITS, PAD, ALU.logical_shift_right, ALU.bitwise_and
                              ).then_inc(unpacked, 1)
            dve.tensor_scalar(field[1][:], bits, PAD, None, ALU.bitwise_and).then_inc(unpacked, 1)
            dve.wait_ge(unpacked, 1)
            dve.tensor_copy(mem.src_sorted[:], field[0][:])
            dve.wait_ge(unpacked, 2)
            dve.tensor_copy(mem.dst_sorted[:], field[1][:])


def make_search(nc, ctx, semaphore, s, mem, n, buffers):
    def sems(name):
        return [semaphore(f"search{n}_{name}{k}") for k in range(buffers)]

    def sbs(name, shape, dt=F32):
        return [ctx.enter_context(nc.sbuf_tensor(f"search{n}_{name}{k}", shape, dt)) for k in range(buffers)]

    of = Memory()
    of.mem, of.n, of.groups = mem, n, s.rows * CH
    of.heads_counted, of.doubled, of.index_made, of.fetched, of.row_counted = (
        sems("heads_counted"), sems("doubled"), sems("index_made"), sems("fetched"), sems("row_counted"))
    of.passed = semaphore(f"search{n}_passed")
    of.head_signs, of.row_signs = sbs("head_signs", [P, of.groups]), sbs("row_signs", [P, GROUP])
    of.balance, of.twice_group = sbs("balance", [P, 1]), sbs("twice_group", [P, 1])
    of.index, of.fetch = sbs("index", [P, 1], I32), sbs("fetch", [P, GROUP])
    return of


def count_heads(of, act, t, k, u):
    reach(act, of.index_made[k], u)
    act.sem_inc(of.passed, 1)
    act.activation(of.head_signs[k][:], of.mem.heads[of.n][:], ACT.Sign, scale=-1.0,
                   bias=of.mem.node_half[:, bass.ds(t, 1)], accum_out=of.balance[k][:]
                   ).then_inc(of.heads_counted[k], 1)


def fetch_group(of, pool, t, k, u):
    pool.wait_ge(of.heads_counted[k], u + 1)
    reach(pool, of.row_counted[k], u)
    pool.sem_inc(of.passed, 1)
    pool.tensor_scalar(of.twice_group[k][:], of.balance[k][:], float(2 - of.groups),
                       float(of.groups - 2), ALU.max, ALU.add).then_inc(of.doubled[k], 1)
    pool.wait_ge(of.doubled[k], u + 1)
    pool.sem_inc(of.passed, 1)
    pool.tensor_scalar(of.index[k][:], of.twice_group[k][:], 0.5, 0.0, ALU.mult, ALU.add
                       ).then_inc(of.index_made[k], 1)
    pool.tensor_copy(of.mem.twice_group[of.n][:, bass.ds(t, 1)], of.twice_group[k][:])
    pool.wait_ge(of.index_made[k], u + 1)
    pool.sem_inc(of.passed, 1)
    pool.indirect_dma_start(of.fetch[k][:], None, of.mem.segment_dram[of.n],
                            bass.IndirectOffsetOnAxis(of.index[k][:], 0)).then_inc(of.fetched[k], 16)


def count_row(of, act, t, k, u):
    act.wait_ge(of.fetched[k], (u + 1) * 16)
    act.sem_inc(of.passed, 1)
    act.activation(of.row_signs[k][:], of.fetch[k][:], ACT.Sign, scale=-1.0,
                   bias=of.mem.node_half[:, bass.ds(t, 1)],
                   accum_out=of.mem.row_balance[of.n][:, bass.ds(t, 1)]).then_inc(of.row_counted[k], 1)


def find_ends(nc, s, mem, n):
    with phase(nc) as (ctx, semaphore):
        def sem(name):
            return semaphore(f"ends{n}_{name}")

        def sb(name):
            return ctx.enter_context(nc.sbuf_tensor(f"ends{n}_{name}", [P, s.tiles], F32))

        step, ended, begun = sem("step"), sem("ended"), sem("begun")
        group_start, in_group, count, some, inverse = (
            sb(x) for x in ("group_start", "in_group", "count", "some", "inverse"))
        begin_bank = ctx.enter_context(nc.psum_tensor(f"ends{n}_begin", [P, P], F32))
        block = ctx.enter_context(nc.Block())
        ends = mem.ends[n]

        @block.tensor
        def _(pe):
            pe.wait_ge(ended, 1)
            pe.matmul(begin_bank[:, 0:s.tiles], mem.ident_wide[:, 0:P], ends[:, 1:1 + s.tiles],
                      start=True, stop=False)
            pe.matmul(begin_bank[:, 0:s.tiles], mem.ident_wide[:, P:2 * P], ends[:, 0:s.tiles],
                      start=False, stop=True).then_inc(begun, 1)

        @block.vector
        def _(dve):
            dve.tensor_scalar(group_start[:], mem.twice_group[n][:], GROUP / 2.0, None, ALU.mult).then_inc(step, 1)
            dve.tensor_scalar(in_group[:], mem.row_balance[n][:], float(GROUP), 0.5, ALU.add, ALU.mult
                              ).then_inc(step, 1)
            dve.wait_ge(step, 2)
            dve.tensor_tensor(ends[:, 1:], group_start[:], in_group[:], ALU.add).then_inc(ended, 1)
            dve.wait_ge(ended, 1)
            dve.tensor_scalar(mem.last[n][:], ends[:, 1:], -1.0, 0.0, ALU.add, ALU.max)
            dve.wait_ge(begun, 1)
            dve.tensor_tensor(count[:], ends[:, 1:], begin_bank[:, 0:s.tiles], ALU.subtract).then_inc(step, 1)
            dve.wait_ge(step, 3)
            some_to = mem.scale[0] if n == 0 else some
            dve.tensor_scalar(some_to[:], count[:], 1.0, None, ALU.min).then_inc(step, 1)
            if n == 1:
                dve.tensor_scalar(count[:], count[:], 1.0, None, ALU.max).then_inc(step, 1)
                dve.wait_ge(step, 5)
                dve.reciprocal(inverse[:], count[:]).then_inc(step, 1)
                dve.wait_ge(step, 6)
                dve.tensor_tensor(mem.scale[1][:], inverse[:], some[:], ALU.mult)




def node_statistics(nc, s, mem):
    with phase(nc) as (ctx, semaphore):
        def sem(name):
            return semaphore(f"statistics_{name}")

        measured, moments_made, collected, rooted, inverted, passed = (
            sem(x) for x in ("measured", "moments_made", "collected", "rooted", "inverted", "passed"))
        statistics = ctx.enter_context(nc.sbuf_tensor("statistics", [P, BATCH, 6], F32))
        moments = ctx.enter_context(nc.sbuf_tensor("moments", [P, BATCH, 2], F32))
        mean = ctx.enter_context(nc.sbuf_tensor("mean", [P, s.tiles], F32))
        variance = ctx.enter_context(nc.sbuf_tensor("variance", [P, s.tiles], F32))
        root = ctx.enter_context(nc.sbuf_tensor("root", [P, s.tiles], F32))
        block = ctx.enter_context(nc.Block())
        batches = s.tiles // BATCH

        @block.vector
        def _(dve):
            def batch(b):
                reach(dve, collected, b * 2)
                dve.sem_inc(passed, 1)
                for t in range(BATCH):
                    dve.bn_stats(statistics[:, t, :], mem.x[:, bass.ds(b * (BATCH * s.d) + t * s.d, s.d)]
                                 ).then_inc(measured, 1)
                dve.wait_ge(measured, (b + 1) * BATCH)
                dve.sem_inc(passed, 1)
                for t in range(BATCH):
                    dve.bn_aggr(moments[:, t, :], statistics[:, t, :]).then_inc(moments_made, 1)
                dve.wait_ge(moments_made, (b + 1) * BATCH)
                dve.sem_inc(passed, 1)
                for to, part in ((mean, 0), (variance, 1)):
                    dve.tensor_copy(to[:, bass.ds(b * BATCH, BATCH)], moments[:, :, part]).then_inc(collected, 1)
            batch(0)
            with dve.Fori(1, batches) as b:
                batch(b)
            dve.wait_ge(rooted, 1)
            dve.reciprocal(mem.inverse_root[:], root[:]).then_inc(inverted, 1)
            dve.wait_ge(inverted, 1)
            dve.scalar_tensor_tensor(mem.shift[:], mean[:], -1.0, mem.inverse_root[:], ALU.mult, ALU.mult)

        @block.scalar
        def _(act):
            act.wait_ge(collected, 2 * batches)
            act.activation(root[:], variance[:], ACT.Sqrt, bias=mem.eps[:, 0:1]).then_inc(rooted, 1)


def sort_and_first_nodes(nc, s, mem):
    D = s.d
    with phase(nc) as (ctx, semaphore):
        keys_made, signs_made, compared, merged, turned, emptied = (
            semaphore(x) for x in ("keys_made", "signs_made", "compared", "merged", "turned", "emptied"))
        h_ready, h_turned, hT_ready, own_ready, own_copied, own_added = (
            semaphore(x) for x in ("h_ready", "h_turned", "hT_ready", "own_ready", "own_copied", "own_added"))
        z_made, z_copied, passed = semaphore("z_made"), semaphore("z_copied"), semaphore("first_nodes_passed")
        z_stored = [semaphore(f"z_stored{k}") for k in range(2)]
        banks = [ctx.enter_context(nc.psum_tensor(f"turned_keys{n}", [P, 4 * P], F32)) for n in range(2)]
        h_bank = ctx.enter_context(nc.psum_tensor("h_bank", [P, 8, P], F32))
        own_bank = ctx.enter_context(nc.psum_tensor("own_bank", [P, 8, D], F32))
        z_bank = [ctx.enter_context(nc.psum_tensor(f"z_bank{n}", [P, s.hid], F32)) for n in range(2)]

        def sb(name, shape, dt=F32):
            return ctx.enter_context(nc.sbuf_tensor(name, shape, dt))

        bit, sign, flip = sb("bit", [P, P], I32), sb("sign", [P, 8, P]), sb("flip", [P, 8, P])
        odd, odd_sign = sb("odd", [P, 1], I32), sb("odd_sign", [P, 1])
        h, hT, own = sb("h0", [P, BATCH, D]), sb("hT0", [P, BATCH, P]), sb("own0", [P, BATCH * D])
        z = sb("z0", [P, 2, BATCH, s.hid])
        search = make_search(nc, ctx, semaphore, s, mem, 1, 2)
        block = ctx.enter_context(nc.Block())
        row_levels = ROW.bit_length() - 1
        merges_over_rows = P.bit_length() - 1
        keys = (mem.key_a, mem.key_b)
        row_steps = row_levels * (row_levels + 1) // 2
        pairs = s.tiles // (2 * BATCH)
        assert s.tiles == pairs * 2 * BATCH

        def over_batches(eng, step):
            for k in range(2):
                step(k, k, 0)
            with eng.Fori(1, pairs) as u:
                for k in range(2):
                    step(u * 2 + k, k, u)

        @block.tensor
        def _(pe):
            def nodes(b, k, u):
                pe.wait_ge(h_ready, b + 1)
                reach(pe, hT_ready, b)
                for t in range(BATCH):
                    turn = pe.transpose(h_bank[:, t, :], h[:, t, :], mem.ident)
                turn.then_inc(h_turned, 1)
                pe.wait_ge(hT_ready, b + 1)
                reach(pe, own_copied, b)
                for t in range(BATCH):
                    mm = pe.matmul(own_bank[:, t, :], hT[:, t, :], mem.w_own[:], start=True, stop=True)
                mm.then_inc(own_ready, 1)
                for t in range(BATCH):
                    reach(pe, z_copied, b * BATCH + (t - 1 if t >= 2 else 0))
                    pe.matmul(z_bank[t % 2][:], hT[:, t, :], mem.fc_w[:], start=True, stop=True
                              ).then_inc(z_made, 1)

            over_batches(pe, nodes)

            steps, turns = row_steps, 0
            for m in range(1, merges_over_rows + 1):
                for following in (1 + m, 1 + row_levels):
                    pe.wait_ge(merged, 2 * (turns + 1))
                    for q in range(4):
                        if q >= 2:
                            pe.wait_ge(emptied, 4 * turns + q - 1)
                        for b in range(4):
                            c = (q * 4 + b) * P
                            turn = pe.transpose(banks[q % 2][:, b * P:(b + 1) * P],
                                                keys[steps % 2][:, c:c + P], mem.ident)
                        turn.then_inc(turned, 1)
                    steps += following
                    turns += 1

        @block.scalar
        def _(act):
            def nodes(b, k, u):
                reach(act, h_turned, b)
                act.sem_inc(passed, 1)
                for t in range(BATCH):
                    column = bass.ds(b * BATCH + t, 1)
                    relu = act.activation(h[:, t, :], mem.x[:, bass.ds(b * (BATCH * D) + t * D, D)], ACT.Relu,
                                          bias=mem.shift[:, column], scale=mem.inverse_root[:, column])
                relu.then_inc(h_ready, 1)
                act.wait_ge(h_turned, b + 1)
                reach(act, z_made, b * BATCH)
                act.copy(hT[:], h_bank[:, 0:BATCH, :]).then_inc(hT_ready, 1)
                act.wait_ge(own_ready, b + 1)
                reach(act, own_added, b)
                act.copy(own[:], own_bank[:, 0:BATCH, :].rearrange("p t d -> p (t d)")).then_inc(own_copied, 1)
                reach(act, z_stored[k], u * 16)
                for t in range(BATCH):
                    act.wait_ge(z_made, b * BATCH + (t + 1))
                    act.copy(z[:, k, t, :], z_bank[t % 2][:]).then_inc(z_copied, 1)

            over_batches(act, nodes)
            for k in range(2):
                count_heads(search, act, k, k, 0)
            with act.Fori(1, s.tiles // 2) as u:
                for k in range(2):
                    count_heads(search, act, u * 2 + k, k, u)
                    count_row(search, act, u * 2 + (k - 2), k, u - 1)
            for k in range(2):
                count_row(search, act, s.tiles - 2 + k, k, s.tiles // 2 - 1)

        @block.gpsimd
        def _(pool):
            def nodes(b, k, u):
                pool.wait_ge(own_copied, b + 1)
                pool.sem_inc(passed, 1)
                x = mem.x[:, bass.ds(b * (BATCH * D), BATCH * D)]
                pool.tensor_tensor(x, x, own[:], ALU.add).then_inc(own_added, 1)

            over_batches(pool, nodes)
            for k in range(2):
                fetch_group(search, pool, k, k, 0)
            with pool.Fori(1, s.tiles // 2) as u:
                for k in range(2):
                    fetch_group(search, pool, u * 2 + k, k, u)

        @block.sync
        def _(sp):
            def nodes(b, k, u):
                sp.wait_ge(z_copied, (b + 1) * BATCH)
                sp.dma_start(mem.z_dram[bass.ds(b * (BATCH * P), BATCH * P), :].rearrange("(t p) f -> p t f", p=P),
                             z[:, k]).then_inc(z_stored[k], 16)

            over_batches(sp, nodes)
            for k in range(2):
                sp.wait_ge(z_stored[k], pairs * 16)

        @block.vector
        def _(dve):
            n = 0
            turns = 0

            def halves(a, stride, mirrored=False):
                v = a[:].rearrange("p (g two j) -> p g two j", two=2, j=stride)
                return v[:, :, 0, :], v[:, :, 1, ::-1] if mirrored else v[:, :, 1, :]

            def compare(step, stride, mirrored=False, last=False):
                nonlocal n
                low, high = halves(keys[step % 2], stride, mirrored)
                low_to, high_to = halves(keys[(step + 1) % 2], stride, mirrored)
                done = merged if last else compared
                dve.tensor_tensor(low_to, low, high, ALU.min).then_inc(done, 1)
                dve.tensor_tensor(high_to, low, high, ALU.max).then_inc(done, 1)
                if not last:
                    n += 2
                    dve.wait_ge(compared, n)

            for m in range(0, 8):
                dve.tensor_scalar(bit[:], mem.row_number[:], m, 1, ALU.logical_shift_right, ALU.bitwise_and
                                  ).then_inc(signs_made, 1)
                dve.wait_ge(signs_made, 2 * m + 1)
                dve.tensor_scalar(sign[:, m, :], bit[:], -2.0, 1.0, ALU.mult, ALU.add).then_inc(signs_made, 1)
                dve.wait_ge(signs_made, 2 * m + 2)
            dve.tensor_tensor(flip[:, 1:8, :], sign[:, 1:8, :], sign[:, 0:7, :], ALU.mult).then_inc(signs_made, 1)
            dve.tensor_scalar(odd[:], mem.partition_number[:], 1, None, ALU.bitwise_and).then_inc(signs_made, 1)
            dve.wait_ge(signs_made, 18)
            dve.tensor_scalar(odd_sign[:], odd[:], -2.0, 1.0, ALU.mult, ALU.add).then_inc(signs_made, 1)

            key_bits = mem.key_b[:].bitcast(I32)
            dve.tensor_scalar(key_bits, mem.src_rows[:], NODE_BITS, ONE_BIT, ALU.logical_shift_left,
                              ALU.bitwise_or).then_inc(keys_made, 1)
            dve.wait_ge(keys_made, 1)
            dve.tensor_tensor(key_bits, key_bits, mem.dst_rows[:], ALU.bitwise_or).then_inc(keys_made, 1)
            dve.wait_ge(keys_made, 2)
            dve.wait_ge(signs_made, 19)
            dve.tensor_scalar(mem.key_a[:], mem.key_b[:], odd_sign[:, 0:1], None, ALU.mult).then_inc(keys_made, 1)
            dve.wait_ge(keys_made, 3)

            step = 0
            for level in range(1, row_levels + 1):
                compare(step, 1 << (level - 1), mirrored=True)
                step += 1
                for j in range(level - 2, -1, -1):
                    compare(step, 1 << j, last=(level == row_levels and j == 0))
                    step += 1
            for m in range(1, merges_over_rows + 1):
                for strides, signed in ((m, True), (row_levels, False)):
                    for q in range(4):
                        dve.wait_ge(turned, 4 * turns + q + 1)
                        to = keys[(step + 1) % 2][:, q * GROUP:(q + 1) * GROUP]
                        if signed:
                            dve.tensor_tensor(to.rearrange("p (b r) -> p b r", r=P),
                                              banks[q % 2][:].rearrange("p (b r) -> p b r", r=P),
                                              flip[:, m:m + 1, :].to_broadcast([P, 4, P]),
                                              ALU.mult).then_inc(emptied, 1)
                        else:
                            dve.tensor_copy(to, banks[q % 2][:]).then_inc(emptied, 1)
                    turns += 1
                    dve.wait_ge(emptied, 4 * turns)
                    step += 1
                    for j in range(strides - 1, -1, -1):
                        compare(step, 1 << j, last=j == 0)
                        step += 1
            assert keys[step % 2] is mem.sorted_keys


def before(r, ch, n):
    return (r, ch - n) if ch >= n else (r - 1, ch + CH - n)


def of_two(r, ch):
    return r * (CH // 2) + ch // 2


def over_groups(eng, step, rows, tail):
    def row(r, chunks):
        for ch in chunks:
            def lagged(f, n):
                if not isinstance(r, int) or r > 0 or ch >= n:
                    f(*before(r, ch, n))
            step(r, ch, lagged)
    row(0, range(CH))
    assert (rows - 1) % UNROLL == 0
    with eng.Fori(0, (rows - 1) // UNROLL) as i:
        for k in range(UNROLL):
            row(i * UNROLL + (k + 1), range(CH))
    row(rows, range(tail))


def is_group(r, ch, *those):
    return isinstance(r, int) and (r, ch) in those


def gather_group(pool, table, index, column, staged, rows, copied, copies, begun, landed):
    pool.tensor_copy(staged, index[:, bass.ds(column, J)]).then_inc(copied, 1)
    pool.wait_ge(copied, copies)
    pool.sem_inc(begun, 1)
    for j in range(J):
        pool.indirect_dma_start(rows[:, j, :], None, table, bass.IndirectOffsetOnAxis(staged[:, j:j + 1], 0)
                                ).then_inc(landed, 16)


def result_rows(dram, g):
    return dram[bass.ds(g * GROUP, GROUP), :].rearrange("(p j) d -> p (j d)", j=J)


def edges_of_layer0(nc, s, mem):
    D, C, H = s.d, s.chunks, s.hid
    with phase(nc) as (ctx, semaphore):
        def sems(name, n):
            return [semaphore(f"e0_{name}{k}") for k in range(n)]

        def sb(name, shape, dt=F32):
            return ctx.enter_context(nc.sbuf_tensor("e0_" + name, shape, dt))

        copied, begun, relu_done = sems("copied", 1)[0], sems("begun", 1)[0], sems("relu_done", 1)[0]
        landed = sems("landed", CH)
        mask_landed = sems("mask_landed", CH)
        z_ready, scanned = sems("z_ready", C), sems("scanned", C)
        y_ready, y_copied, stored = sems("y_ready", 1)[0], sems("y_copied", 2), sems("stored", 2)

        staged = sb("staged", [P, CH, J], I32)
        rows = [sb(f"rows{k}", [P, J, H]) for k in range(CH)]
        mask = sb("mask", [P, CH, GROUP], BF16)
        best = sb("best", [P, 2, C, GROUP])
        agg = sb("agg", [P, 2, C, GROUP])
        y = sb("y", [P, 2, J * D])
        z = [ctx.enter_context(nc.psum_tensor(f"e0_z{c}", [P, GROUP], F32)) for c in range(C)]
        y_bank = [ctx.enter_context(nc.psum_tensor(f"e0_y_bank{k}", [P, J * D], F32)) for k in range(2)]
        search = make_search(nc, ctx, semaphore, s, mem, 0, 1)
        block = ctx.enter_context(nc.Block())

        def over_all(eng, step):
            over_groups(eng, step, s.rows - 1, CH)

        @block.gpsimd
        def _(pool):
            def step(r, ch, lagged):
                if not (isinstance(r, int) and r == 0):
                    pool.wait_ge(z_ready[C - 1], (r - 1) * CH + (ch + 1))
                gather_group(pool, mem.z_dram, mem.index[0], r * (CH * J) + ch * J, staged[:, ch, :],
                             rows[ch], copied, r * CH + (ch + 1), begun, landed[ch])
                if ch == 1 and not (isinstance(r, int) and r == 0):
                    fetch_group(search, pool, r - 1, 0, r - 1)
            over_all(pool, step)
            fetch_group(search, pool, s.rows - 1, 0, s.rows - 1)

        @block.tensor
        def _(pe):
            def turn(r, ch, c):
                if c == 0:
                    pe.wait_ge(landed[ch], (r + 1) * (16 * J))
                reach(pe, scanned[c], r * CH + ch)
                for j in range(J):
                    t = pe.transpose(z[c][:, j::J], rows[ch][:, j, c * P:(c + 1) * P], mem.ident)
                t.then_inc(z_ready[c], 1)

            def project(r, ch, j):
                k = ch % 2
                if j == 0:
                    pe.wait_ge(relu_done, (r * CH + (ch + 1)) * C)
                    reach(pe, y_copied[k], of_two(r, ch))
                for c in range(C):
                    mm = pe.matmul(y_bank[k][:, j * D:(j + 1) * D], agg[:, k, c, j::J], mem.w_agg[:, c, :],
                                   start=c == 0, stop=c == C - 1)
                if j == J - 1:
                    mm.then_inc(y_ready, 1)

            def step(r, ch, lagged):
                for c in range(C):
                    turn(r, ch, c)
                    lagged(lambda r2, ch2: project(r2, ch2, c), 2)
            over_all(pe, step)
            for n in (2, 1):
                for j in range(J):
                    project(*before(s.rows, 0, n), j)

        @block.scalar
        def _(act):
            def rectify(r, ch):
                if not is_group(r, ch, (0, 0), (0, 1)):
                    r2, ch2 = before(r, ch, 2)
                    act.wait_ge(y_ready, r2 * CH + (ch2 + 1))
                for c in range(C):
                    act.wait_ge(scanned[c], r * CH + (ch + 1))
                    act.activation(agg[:, ch % 2, c, :], best[:, ch % 2, c, :], ACT.Relu,
                                   bias=mem.fc_b[:, c:c + 1]).then_inc(relu_done, 1)

            def copy_y(r, ch):
                k = ch % 2
                act.wait_ge(y_ready, r * CH + (ch + 1))
                reach(act, stored[k], of_two(r, ch) * 16)
                act.copy(y[:, k, :], y_bank[k][:]).then_inc(y_copied[k], 1)

            def step(r, ch, lagged):
                lagged(copy_y, 3)
                lagged(rectify, 1)
                if ch == 0:
                    count_heads(search, act, r, 0, r)
                elif ch == 2 and not (isinstance(r, int) and r == 0):
                    count_row(search, act, r - 1, 0, r - 1)
            over_all(act, step)
            rectify(*before(s.rows, 0, 1))
            for n in (3, 2, 1):
                copy_y(*before(s.rows, 0, n))
            count_row(search, act, s.rows - 1, 0, s.rows - 1)

        @block.vector
        def _(dve):
            def step(r, ch, lagged):
                k = ch % 2
                dve.wait_ge(mask_landed[ch], (r + 1) * 16)
                for c in range(C):
                    dve.wait_ge(z_ready[c], r * CH + (ch + 1))
                    if is_group(r, ch, (0, 0)):
                        state = RESET
                    else:
                        dve.wait_ge(scanned[c], r * CH + ch)
                        state = best[:, 1 - k, c, GROUP - 1:GROUP]
                    if not is_group(r, ch, (0, 0), (0, 1)):
                        r2, ch2 = before(r, ch, 2)
                        dve.wait_ge(relu_done, (r2 * CH + ch2) * C + (c + 1))
                    dve.tensor_tensor_scan(best[:, k, c, :], mask[:, ch, :], z[c][:], state,
                                           ALU.add, ALU.max).then_inc(scanned[c], 1)
            over_all(dve, step)

        @block.sync
        def _(sp):
            def load_mask(r, ch):
                if not (isinstance(r, int) and r == 0):
                    sp.wait_ge(scanned[C - 1], (r - 1) * CH + (ch + 1))
                sp.dma_start(mask[:, ch, :], mem.reset_dram[bass.ds(r * CH + ch, 1), :].to_broadcast([P, GROUP])
                             ).then_inc(mask_landed[ch], 16)

            def store(r, ch):
                sp.wait_ge(y_copied[ch % 2], of_two(r, ch) + 1)
                sp.dma_start(result_rows(mem.result_dram, r * CH + ch), y[:, ch % 2, :]
                             ).then_inc(stored[ch % 2], 16)

            def step(r, ch, lagged):
                load_mask(r, ch)
                lagged(store, 4)
            over_all(sp, step)
            for n in (4, 3, 2, 1):
                store(*before(s.rows, 0, n))
            for k in range(2):
                sp.wait_ge(stored[k], s.rows * (CH // 2) * 16)


def edges_of_layer1(nc, s, mem, edge_attr):
    D = s.d
    with phase(nc) as (ctx, semaphore):
        def sems(name, n=CH):
            return [semaphore(f"e1_{name}{k}") for k in range(n)]

        def sb(name, shape, dt=F32):
            return ctx.enter_context(nc.sbuf_tensor("e1_" + name, shape, dt))

        staged_ready, begun = sems("staged_ready"), semaphore("e1_begun")
        landed, attr_landed, attr_turned, z_ready = (
            sems("landed"), sems("attr_landed"), sems("attr_turned"), sems("z_ready"))
        attrT_ready, mask_ready, relu_done = sems("attrT_ready", 2), sems("mask_ready", 2), sems("relu_done", 2)
        mask_spread = sems("mask_spread", 1)[0]
        scanned, back_turned, sums_ready, stored = (
            sems("scanned"), sems("back_turned"), sems("sums_ready"), sems("stored"))
        tail_cleared, passed = semaphore("e1_tail_cleared"), semaphore("e1_passed")

        staged = sb("staged", [P, CH, J], I32)
        rows = sb("rows", [P, CH, J, D])
        attr = sb("attr", [P, CH, J * D])
        attrT = sb("attrT", [P, 2, GROUP])
        mask = sb("mask", [P, 2, GROUP], BF16)
        message = sb("message", [P, 2, GROUP])
        total = sb("total", [P, CH, GROUP])
        sums = sb("sums", [P, CH, J * D])
        turned = [ctx.enter_context(nc.psum_tensor(f"e1_turned{k}", [P, GROUP], F32)) for k in range(2)]
        mask_bank = ctx.enter_context(nc.psum_tensor("e1_mask_bank", [P, GROUP], F32))
        z = [ctx.enter_context(nc.psum_tensor(f"e1_z{k}", [P, GROUP], F32)) for k in range(2)]
        back = [ctx.enter_context(nc.psum_tensor(f"e1_back{k}", [P, J * D], F32)) for k in range(2)]
        block = ctx.enter_context(nc.Block())
        tail = s.groups - s.full_rows * CH
        tail_rows = (s.edges % GROUP) // J
        assert tail_rows * J == s.edges % GROUP and 0 < tail_rows and 0 < tail < CH
        last_row = s.full_rows

        def over_rows(eng, step):
            over_groups(eng, step, last_row, tail)

        @block.gpsimd
        def _(pool):
            def step(r, ch, lagged):
                pool.wait_ge(staged_ready[ch], r + 1)
                pool.sem_inc(begun, 1)
                for j in range(J):
                    pool.indirect_dma_start(rows[:, ch, j, :], None, mem.message_dram,
                                            bass.IndirectOffsetOnAxis(staged[:, ch, j:j + 1], 0)
                                            ).then_inc(landed[ch], 16)
            over_rows(pool, step)

        @block.sync
        def _(sp):
            def step(r, ch, lagged):
                if isinstance(r, int) and (r, ch) == (last_row, tail - 1):
                    sp.wait_ge(tail_cleared, 1)
                    sp.dma_start(attr[0:tail_rows, ch, :],
                                 edge_attr[(r * CH + ch) * GROUP:s.edges, :].rearrange("(p j) d -> p (j d)", j=J)
                                 ).then_inc(attr_landed[ch], 16)
                else:
                    reach(sp, attr_turned[ch], r)
                    sp.dma_start(attr[:, ch, :], result_rows(edge_attr, r * CH + ch)
                                 ).then_inc(attr_landed[ch], 16)
            over_rows(sp, step)
            for ch in range(CH):
                sp.wait_ge(stored[ch], (last_row + (ch < tail)) * 16)

        @block.tensor
        def _(pe):
            def turn(r, ch):
                k = ch % 2
                pe.wait_ge(attr_landed[ch], (r + 1) * 16)
                reach(pe, attrT_ready[k], of_two(r, ch))
                for j in range(J):
                    t = pe.transpose(turned[k][:, j::J], attr[:, ch, j * D:(j + 1) * D], mem.ident)
                t.then_inc(attr_turned[ch], 1)
                last = before(r, ch, 1) if not (isinstance(r, int) and r == 0 and ch == 0) else None
                if last:
                    pe.wait_ge(mask_ready[last[1] % 2], of_two(*last) + 1)
                pe.matmul(mask_bank[:], mem.ident_bf[:, bass.ds(r, 1)].to_broadcast([P, P]),
                          mem.resets[1][:, ch * GROUP:(ch + 1) * GROUP], start=True, stop=True
                          ).then_inc(mask_spread, 1)

            def combine(r, ch):
                k = ch % 2
                pe.wait_ge(attrT_ready[k], of_two(r, ch) + 1)
                pe.wait_ge(landed[ch], (r + 1) * (16 * J))
                reach(pe, relu_done[k], of_two(r, ch))
                pe.matmul(z[k][:], mem.wm_attr[:], attrT[:, k, :], start=True, stop=False)
                for j in range(J):
                    mm = pe.matmul(z[k][:, j::J], rows[:, ch, j, :], mem.ident, start=False, stop=j == J - 1)
                mm.then_inc(z_ready[ch], 1)

            def turn_back(r, ch):
                pe.wait_ge(scanned[ch], r + 1)
                if not (isinstance(r, int) and r == 0 and ch < 2):
                    r2, ch2 = before(r, ch, 2)
                    pe.wait_ge(sums_ready[ch2], r2 + 1)
                for j in range(J):
                    t = pe.transpose(back[ch % 2][:, j * D:(j + 1) * D], total[:, ch, j::J], mem.ident)
                t.then_inc(back_turned[ch], 1)

            def step(r, ch, lagged):
                turn(r, ch)
                lagged(combine, 1)
                lagged(turn_back, 3)
            over_rows(pe, step)
            combine(last_row, tail - 1)
            for n in (3, 2, 1):
                turn_back(*before(last_row, tail, n))

        @block.scalar
        def _(act):
            def spread(r, ch):
                k = ch % 2
                act.wait_ge(attr_turned[ch], r + 1)
                if not (isinstance(r, int) and r == 0 and ch < 2):
                    r2, ch2 = before(r, ch, 2)
                    act.wait_ge(scanned[ch2], r2 + 1)
                act.copy(attrT[:, k, :], turned[k][:]).then_inc(attrT_ready[k], 1)
                act.wait_ge(mask_spread, r * CH + (ch + 1))
                act.copy(mask[:, k, :], mask_bank[:]).then_inc(mask_ready[k], 1)

            def rectify(r, ch):
                act.wait_ge(z_ready[ch], r + 1)
                act.activation(message[:, ch % 2, :], z[ch % 2][:], ACT.Relu, bias=mem.b_msg[:, 0:1]
                               ).then_inc(relu_done[ch % 2], 1)

            def store(r, ch):
                act.wait_ge(sums_ready[ch], r + 1)
                act.dma_start(result_rows(mem.result_dram, r * CH + ch), sums[:, ch, :]).then_inc(stored[ch], 16)

            def step(r, ch, lagged):
                spread(r, ch)
                lagged(rectify, 1)
                lagged(store, 4)
            over_rows(act, step)
            rectify(last_row, tail - 1)
            for n in (4, 3, 2, 1):
                store(*before(last_row, tail, n))

        @block.vector
        def _(dve):
            def scan(r, ch):
                k = ch % 2
                dve.wait_ge(mask_ready[k], of_two(r, ch) + 1)
                dve.wait_ge(relu_done[k], of_two(r, ch) + 1)
                reach(dve, back_turned[ch], r)
                if isinstance(r, int) and (r, ch) == (0, 0):
                    state = 0.0
                else:
                    r1, ch1 = before(r, ch, 1)
                    dve.wait_ge(scanned[ch1], r1 + 1)
                    state = total[:, ch1, GROUP - 1:GROUP]
                dve.tensor_tensor_scan(total[:, ch, :], mask[:, k, :], message[:, k, :], state,
                                       ALU.mult, ALU.add).then_inc(scanned[ch], 1)

            def empty(r, ch):
                dve.wait_ge(back_turned[ch], r + 1)
                reach(dve, stored[ch], r * 16)
                dve.tensor_copy(sums[:, ch, :], back[ch % 2][:]).then_inc(sums_ready[ch], 1)

            def stage_indices(r, ch):
                reach(dve, z_ready[ch], r)
                dve.sem_inc(passed, 1)
                dve.tensor_copy(staged[:, ch, :], mem.index[1][:, bass.ds(r * (CH * J) + ch * J, J)]
                                ).then_inc(staged_ready[ch], 1)

            for ch in range(CH):
                stage_indices(0, ch)

            def step(r, ch, lagged):
                if not isinstance(r, int) or r + 1 < last_row or (r + 1 == last_row and ch < tail):
                    stage_indices(r + 1, ch)
                if isinstance(r, int) and (r, ch) == (last_row, 0):
                    dve.wait_ge(attr_turned[tail - 1], last_row)
                    dve.memset(attr[:, tail - 1, :], 0.0).then_inc(tail_cleared, 1)
                scan(r, ch)
                lagged(empty, 3)
            over_rows(dve, step)
            for n in (3, 2, 1):
                empty(*before(last_row, tail, n))




def over_batches(eng, s, step):
    pairs = s.tiles // (2 * BATCH)

    def one(b, k, u):
        def lagged(f):
            if not isinstance(b, int) or b > 0:
                f(b - 1, 1 - k, u if k else u - 1)
        step(b, k, u, lagged)
    for k in range(2):
        one(k, k, 0)
    with eng.Fori(1, pairs) as u:
        for k in range(2):
            one(u * 2 + k, k, u)


def last_batch(s):
    batches = s.tiles // BATCH
    return batches - 1, 1, batches // 2 - 1


def make_norm(nc, ctx, semaphore, mem, name):
    norm = Memory()
    norm.eps = mem.eps
    norm.measured, norm.moments_made, norm.rooted, norm.inverted, norm.passed = (
        semaphore(f"{name}_{x}") for x in ("measured", "moments_made", "rooted", "inverted", "passed"))
    norm.statistics = ctx.enter_context(nc.sbuf_tensor(f"{name}_statistics", [P, BATCH, 6], F32))
    norm.moments = ctx.enter_context(nc.sbuf_tensor(f"{name}_moments", [P, BATCH, 2], F32))
    norm.root = ctx.enter_context(nc.sbuf_tensor(f"{name}_root", [P, BATCH], F32))
    norm.inverse = ctx.enter_context(nc.sbuf_tensor(f"{name}_inverse", [P, BATCH], F32))
    return norm


def measure_rows(norm, dve, b, tile):
    dve.sem_inc(norm.passed, 1)
    for t in range(BATCH):
        dve.bn_stats(norm.statistics[:, t, :], tile(t)).then_inc(norm.measured, 1)
    dve.wait_ge(norm.measured, (b + 1) * BATCH)
    dve.sem_inc(norm.passed, 1)
    for t in range(BATCH):
        dve.bn_aggr(norm.moments[:, t, :], norm.statistics[:, t, :]).then_inc(norm.moments_made, 1)


def take_roots(norm, act, b):
    act.wait_ge(norm.moments_made, (b + 1) * BATCH)
    act.activation(norm.root[:], norm.moments[:, :, 1], ACT.Sqrt, bias=norm.eps[:, 0:1]).then_inc(norm.rooted, 1)


def invert_roots(norm, dve, b):
    dve.wait_ge(norm.rooted, b + 1)
    dve.reciprocal(norm.inverse[:], norm.root[:]).then_inc(norm.inverted, 1)
    dve.wait_ge(norm.inverted, b + 1)


def node_rows(dram, b):
    return dram[bass.ds(b * (BATCH * P), BATCH * P), :].rearrange("(t p) d -> p t d", p=P)


def gather_last_rows(pool, s, last, table, staged, rows, copied, begun, landed, used, b, k, u):
    reach(pool, used[k], u)
    pool.tensor_copy(staged[:, k, :], last[:, bass.ds(b * BATCH, BATCH)]).then_inc(copied, 1)
    pool.wait_ge(copied, b + 1)
    pool.sem_inc(begun, 1)
    for t in range(BATCH):
        pool.indirect_dma_start(rows[:, k, t, :], None, table,
                                bass.IndirectOffsetOnAxis(staged[:, k, t:t + 1], 0)).then_inc(landed[k], 16)


def nodes_between_layers(nc, s, mem):
    D = s.d
    with phase(nc) as (ctx, semaphore):
        norm = make_norm(nc, ctx, semaphore, mem, "norm_b")

        def sem(name):
            return semaphore("between_" + name)

        def sb(name, shape, dt=F32):
            return ctx.enter_context(nc.sbuf_tensor("between_" + name, shape, dt))

        copied, begun, normed, h_ready, h_turned, hT_ready, product_ready, message_ready = (
            sem(x) for x in ("copied", "begun", "normed", "h_ready", "h_turned", "hT_ready", "product_ready",
                             "message_ready"))
        landed, used, message_stored, hT_stored = (
            [sem(f"{x}{k}") for k in range(2)] for x in ("landed", "used", "message_stored", "hT_stored"))
        staged = sb("staged", [P, 2, BATCH], I32)
        rows, h, message = sb("rows", [P, 2, BATCH, D]), sb("h", [P, 2, BATCH, D]), sb("message", [P, 2, BATCH, D])
        hT = sb("hT", [P, 2, BATCH * P])
        turned = ctx.enter_context(nc.psum_tensor("between_turned", [P, 8 * P], F32))
        product = ctx.enter_context(nc.psum_tensor("between_product", [P, 8, D], F32))
        block = ctx.enter_context(nc.Block())

        @block.gpsimd
        def _(pool):
            over_batches(pool, s, lambda b, k, u, lagged: gather_last_rows(
                pool, s, mem.last[0], mem.result_dram, staged, rows, copied, begun, landed, used, b, k, u))

        @block.vector
        def _(dve):
            def step(b, k, u, lagged):
                def x_tile(t):
                    return mem.x[:, bass.ds(b * (BATCH * D) + t * D, D)]
                dve.wait_ge(landed[k], (u + 1) * (16 * BATCH))
                dve.sem_inc(norm.passed, 1)
                for t in range(BATCH):
                    add = dve.scalar_tensor_tensor(x_tile(t), rows[:, k, t, :],
                                                   mem.scale[0][:, bass.ds(b * BATCH + t, 1)],
                                                   x_tile(t), ALU.mult, ALU.add)
                add.then_inc(used[k], 1)
                dve.wait_ge(used[k], u + 1)
                measure_rows(norm, dve, b, x_tile)
                if not isinstance(b, int) or b >= 2:
                    dve.wait_ge(h_turned, b - 1)
                invert_roots(norm, dve, b)
                dve.sem_inc(norm.passed, 1)
                for t in range(BATCH):
                    dve.tensor_scalar(h[:, k, t, :], x_tile(t), norm.moments[:, t, 0:1], norm.inverse[:, t:t + 1],
                                      ALU.subtract, ALU.mult).then_inc(normed, 1)
                dve.wait_ge(normed, (b + 1) * BATCH)
                dve.tensor_scalar(h[:, k], h[:, k], 0.0, None, ALU.max).then_inc(h_ready, 1)
                dve.wait_ge(h_ready, b + 1)
                dve.sem_inc(norm.passed, 1)
                dve.tensor_tensor(mem.h_beta[:, bass.ds(b * (BATCH * D), BATCH * D)].rearrange(
                    "p (t d) -> p t d", d=D), h[:, k], mem.beta[:].unsqueeze(1).to_broadcast([P, BATCH, D]), ALU.add)
            over_batches(dve, s, step)

        @block.scalar
        def _(act):
            def copy_message(b, k, u):
                act.wait_ge(product_ready, b + 1)
                reach(act, message_stored[k], u * 16)
                act.copy(message[:, k], product[:, 0:BATCH, :]).then_inc(message_ready, 1)

            def step(b, k, u, lagged):
                take_roots(norm, act, b)
                lagged(copy_message)
                act.wait_ge(h_turned, b + 1)
                reach(act, hT_stored[k], u * 16)
                act.copy(hT[:, k, :], turned[:, 0:BATCH * P]).then_inc(hT_ready, 1)
            over_batches(act, s, step)
            copy_message(*last_batch(s))

        @block.tensor
        def _(pe):
            def step(b, k, u, lagged):
                pe.wait_ge(h_ready, b + 1)
                reach(pe, hT_ready, b)
                for t in range(BATCH):
                    turn = pe.transpose(turned[:, t * P:(t + 1) * P], h[:, k, t, :], mem.ident)
                turn.then_inc(h_turned, 1)
                pe.wait_ge(hT_ready, b + 1)
                reach(pe, message_ready, b)
                for t in range(BATCH):
                    mm = pe.matmul(product[:, t, :], hT[:, k, t * P:(t + 1) * P], mem.wm_own[:],
                                   start=True, stop=True)
                mm.then_inc(product_ready, 1)
            over_batches(pe, s, step)

        @block.sync
        def _(sp):
            def store_message(b, k, u):
                sp.wait_ge(message_ready, b + 1)
                sp.dma_start(node_rows(mem.message_dram, b), message[:, k]).then_inc(message_stored[k], 16)

            def step(b, k, u, lagged):
                sp.wait_ge(hT_ready, b + 1)
                sp.dma_start(mem.hT_dram[bass.ds(b * P, P), :], hT[:, k, :]).then_inc(hT_stored[k], 16)
                lagged(store_message)
            over_batches(sp, s, step)
            store_message(*last_batch(s))
            for k in range(2):
                sp.wait_ge(hT_stored[k], s.tiles // (2 * BATCH) * 16)
                sp.wait_ge(message_stored[k], s.tiles // (2 * BATCH) * 16)


def nodes_after_layer1(nc, s, mem, out):
    D = s.d
    with phase(nc) as (ctx, semaphore):
        norm = make_norm(nc, ctx, semaphore, mem, "norm_u")

        def sem(name):
            return semaphore("after_" + name)

        def sb(name, shape, dt=F32):
            return ctx.enter_context(nc.sbuf_tensor("after_" + name, shape, dt))

        copied, begun, mean_ready, mean_turned, meanT_ready, product_ready, scaled, shifted, finished, passed = (
            sem(x) for x in ("copied", "begun", "mean_ready", "mean_turned", "meanT_ready", "product_ready",
                             "scaled", "shifted", "finished", "passed"))
        landed, used, hT_landed, stored = (
            [sem(f"{x}{k}") for k in range(2)] for x in ("landed", "used", "hT_landed", "stored"))
        staged = sb("staged", [P, 2, BATCH], I32)
        rows, mean, meanT, hT = (sb(x, [P, 2, BATCH, D]) for x in ("rows", "mean", "meanT", "hT"))
        centred, summed = sb("centred", [P, BATCH, D]), sb("summed", [P, BATCH * D])
        result = sb("result", [P, 2, BATCH, D])
        turned = ctx.enter_context(nc.psum_tensor("after_turned", [P, 8, P], F32))
        product = [ctx.enter_context(nc.psum_tensor(f"after_product{k}", [P, 8, D], F32)) for k in range(2)]
        block = ctx.enter_context(nc.Block())
        batches = s.tiles // BATCH

        @block.gpsimd
        def _(pool):
            over_batches(pool, s, lambda b, k, u, lagged: gather_last_rows(
                pool, s, mem.last[1], mem.result_dram, staged, rows, copied, begun, landed, used, b, k, u))

        @block.scalar
        def _(act):
            def step(b, k, u, lagged):
                act.wait_ge(landed[k], (u + 1) * (16 * BATCH))
                if not isinstance(b, int) or b >= 2:
                    act.wait_ge(mean_turned, b - 1)
                act.sem_inc(passed, 1)
                for t in range(BATCH):
                    act.activation(mean[:, k, t, :], rows[:, k, t, :], ACT.Copy,
                                   scale=mem.scale[1][:, bass.ds(b * BATCH + t, 1)]).then_inc(mean_ready, 1)
                act.wait_ge(mean_ready, (b + 1) * BATCH)
                act.sem_inc(used[k], 1)
                lagged(lambda b1, k1, u1: take_roots(norm, act, b1))
                act.wait_ge(mean_turned, b + 1)
                if not isinstance(b, int) or b >= 2:
                    act.wait_ge(product_ready, b - 1)
                act.copy(meanT[:, k], turned[:, 0:BATCH, :]).then_inc(meanT_ready, 1)
            over_batches(act, s, step)
            take_roots(norm, act, batches - 1)

        @block.tensor
        def _(pe):
            def step(b, k, u, lagged):
                pe.wait_ge(mean_ready, (b + 1) * BATCH)
                reach(pe, meanT_ready, b)
                for t in range(BATCH):
                    turn = pe.transpose(turned[:, t, :], mean[:, k, t, :], mem.ident)
                turn.then_inc(mean_turned, 1)
                pe.wait_ge(hT_landed[k], (u + 1) * 16)
                if not isinstance(b, int) or b >= 2:
                    pe.wait_ge(scaled, (b - 1) * BATCH)
                pe.wait_ge(meanT_ready, b + 1)
                for t in range(BATCH):
                    pe.matmul(product[k][:, t, :], mem.ones[0:1, :], mem.b_upd[0:1, :], start=True, stop=False)
                    pe.matmul(product[k][:, t, :], hT[:, k, t, :], mem.wu_own[:], start=False, stop=False)
                    mm = pe.matmul(product[k][:, t, :], meanT[:, k, t, :], mem.wu_mean[:], start=False, stop=True)
                mm.then_inc(product_ready, 1)
            over_batches(pe, s, step)

        @block.vector
        def _(dve):
            def step(b, k, u, lagged):
                dve.wait_ge(product_ready, b + 1)
                measure_rows(norm, dve, b, lambda t: product[k][:, t, :])
                invert_roots(norm, dve, b)
                reach(dve, shifted, b * BATCH)
                dve.sem_inc(passed, 1)
                for t in range(BATCH):
                    dve.scalar_tensor_tensor(centred[:, t, :], product[k][:, t, :], norm.moments[:, t, 0:1],
                                             mem.gamma[:], ALU.subtract, ALU.mult).then_inc(scaled, 1)
                dve.wait_ge(scaled, (b + 1) * BATCH)
                reach(dve, finished, b)
                dve.sem_inc(passed, 1)
                for t in range(BATCH):
                    dve.scalar_tensor_tensor(summed[:, t * D:(t + 1) * D], centred[:, t, :],
                                             norm.inverse[:, t:t + 1],
                                             mem.h_beta[:, bass.ds(b * (BATCH * D) + t * D, D)],
                                             ALU.mult, ALU.add).then_inc(shifted, 1)
                dve.wait_ge(shifted, (b + 1) * BATCH)
                reach(dve, stored[k], u * 16)
                dve.sem_inc(passed, 1)
                dve.scalar_tensor_tensor(result[:, k].rearrange("p t d -> p (t d)"), summed[:], 0.0,
                                         mem.x[:, bass.ds(b * (BATCH * D), BATCH * D)], ALU.max, ALU.add
                                         ).then_inc(finished, 1)
            over_batches(dve, s, step)

        @block.sync
        def _(sp):
            def store(b, k, u):
                sp.wait_ge(finished, b + 1)
                sp.dma_start(node_rows(out, b), result[:, k]).then_inc(stored[k], 16)

            def step(b, k, u, lagged):
                if not isinstance(b, int) or b >= 2:
                    sp.wait_ge(product_ready, b - 1)
                sp.dma_start(hT[:, k].rearrange("p t d -> p (t d)"), mem.hT_dram[bass.ds(b * P, P), :]
                             ).then_inc(hT_landed[k], 16)
                lagged(store)
            over_batches(sp, s, step)
            first, full = (batches - 1) * BATCH * P, s.nodes // P - (batches - 1) * BATCH
            sp.wait_ge(finished, batches)
            sp.dma_start(out[first:first + full * P, :].rearrange("(t p) d -> p t d", p=P), result[:, 1, 0:full, :]
                         ).then_inc(stored[1], 16)
            sp.dma_start(out[first + full * P:s.nodes, :], result[0:s.nodes % P, 1, full, :]).then_inc(stored[1], 16)
            sp.wait_ge(stored[0], batches // 2 * 16)
            sp.wait_ge(stored[1], (batches // 2 + 1) * 16)




def gnn_kernel(nc, x, src, dst, edge_attr, fc_w, fc_b, w_layer0, w_msg, b_msg, w_upd, b_upd, gamma, beta, out):
    nodes, d = x.shape
    s = Shapes(nodes, src.shape[0], d, fc_w.shape[1])
    mem = Memory()
    with ExitStack() as ctx:
        def sb(name, shape, dt=F32):
            return ctx.enter_context(nc.sbuf_tensor(name, shape, dt))

        rows = s.tiles * P
        mem.x_dram = x
        mem.z_dram = nc.dram_tensor("z_dram", (rows, s.hid), F32).ap()
        mem.hT_dram = nc.dram_tensor("hT_dram", (s.tiles // BATCH * P, BATCH * P), F32).ap()
        mem.message_dram = nc.dram_tensor("message_dram", (rows, d), F32).ap()
        mem.result_dram = nc.dram_tensor("result_dram", (s.rows * ROW, d), F32).ap()
        mem.reset_dram = nc.dram_tensor("reset_dram", (s.rows * CH, GROUP), BF16).ap()
        mem.segment_dram = [nc.dram_tensor(f"segment_dram{n}", (s.rows * CH, GROUP), F32).ap() for n in range(2)]
        mem.x = sb("x", [P, s.tiles * d])
        mem.ident_wide = sb("ident_wide", [P, 2 * P])
        mem.ident = mem.ident_wide[:, 1:1 + P]
        mem.ident_bf = sb("ident_bf", [P, P], BF16)
        mem.ones = sb("ones", [P, P])
        mem.eps = sb("eps", [P, 1])
        mem.node_number = sb("node_number", [P, s.tiles])
        mem.row_number = sb("row_number", [P, P], I32)
        mem.partition_number = sb("partition_number", [P, 1], I32)
        mem.index = [sb(f"index{n}", [P, ROW], I32) for n in range(2)]
        mem.resets = [sb(f"resets{n}", [P, ROW], BF16) for n in range(2)]
        mem.heads = [sb(f"heads{n}", [P, s.rows * CH]) for n in range(2)]
        mem.twice_group = [sb(f"twice_group{n}", [P, s.tiles]) for n in range(2)]
        mem.row_balance = [sb(f"row_balance{n}", [P, s.tiles]) for n in range(2)]
        mem.ends = [sb(f"ends{n}", [P, 1 + s.tiles]) for n in range(2)]
        mem.last = [sb(f"last{n}", [P, s.tiles], I32) for n in range(2)]
        mem.scale = [sb(f"scale{n}", [P, s.tiles]) for n in range(2)]
        mem.inverse_root = sb("inverse_root", [P, s.tiles])
        mem.shift = sb("shift", [P, s.tiles])
        mem.node_half = sb("node_half", [P, s.tiles])
        mem.fc_w = sb("fc_w", [P, s.hid])
        mem.fc_b = sb("fc_b", [P, s.chunks])
        mem.w_own = sb("w_own", [P, d])
        mem.w_agg = sb("w_agg", [P, s.chunks, d])
        mem.wm_own = sb("wm_own", [P, d])
        mem.wm_attr = sb("wm_attr", [P, d])
        mem.b_msg = sb("b_msg", [P, 1])
        mem.wu_own = sb("wu_own", [P, d])
        mem.wu_mean = sb("wu_mean", [P, d])
        mem.b_upd = sb("b_upd", [P, d])
        mem.gamma = sb("gamma", [P, d])
        mem.beta = sb("beta", [P, d])
        ctx.enter_context(nc.allow_non_contiguous_dma(reason="biases onto partitions, once"))
        mem.weights = [
            (mem.fc_w[:], fc_w),
            (mem.fc_b[:], fc_b.rearrange("(c p) -> p c", p=P)),
            (mem.w_own[:], w_layer0[0:d, :]),
            (mem.w_agg[:], w_layer0[d:, :].rearrange("(c p) n -> p c n", p=P)),
            (mem.wm_own[:], w_msg[0:d, :]),
            (mem.wm_attr[:], w_msg[d:, :]),
            (mem.b_msg[:], b_msg.rearrange("(p a) -> p a", a=1)),
            (mem.wu_own[:], w_upd[0:d, :]),
            (mem.wu_mean[:], w_upd[d:, :]),
            (mem.b_upd[:], b_upd.rearrange("(a d) -> a d", a=1).to_broadcast([P, d])),
            (mem.gamma[:], gamma.rearrange("(a d) -> a d", a=1).to_broadcast([P, d])),
            (mem.beta[:], beta.rearrange("(a d) -> a d", a=1).to_broadcast([P, d])),
        ]
        with ExitStack() as early:
            def rows_of(name, dt=F32):
                return early.enter_context(nc.sbuf_tensor(name, [P, ROW], dt))

            mem.src_rows, mem.dst_rows = rows_of("src_rows", I32), rows_of("dst_rows", I32)
            mem.key_a, mem.key_b = rows_of("key_a"), rows_of("key_b")
            mem.sorted_keys = mem.key_b
            with ExitStack() as given:
                mem.src_given, mem.dst_given = (
                    given.enter_context(nc.sbuf_tensor(f"{x}_given", [P, ROW], F32)) for x in ("src", "dst"))
                setup(nc, s, mem, src, dst)
                make_tables(nc, s, mem, 1, mem.dst_given, mem.src_given, mem.index[1], mem.resets[1], "keep")
            node_statistics(nc, s, mem)
            sort_and_first_nodes(nc, s, mem)
            mem.src_sorted, mem.dst_sorted = rows_of("src_sorted"), rows_of("dst_sorted")
            unpack_sorted_keys(nc, s, mem)
            make_tables(nc, s, mem, 0, mem.src_sorted, mem.dst_sorted, mem.index[0], mem.resets[0], "reset")
        edges_of_layer0(nc, s, mem)
        find_ends(nc, s, mem, 0)
        mem.h_beta = sb("h_beta", [P, s.tiles * d])
        nodes_between_layers(nc, s, mem)
        find_ends(nc, s, mem, 1)
        edges_of_layer1(nc, s, mem, edge_attr)
        nodes_after_layer1(nc, s, mem, out)


_INS = ["x", "src", "dst", "edge_attr_128", "L0_gnn_fc_w", "L0_gnn_fc_b", "L0_gnn_weights_matrix", "L1_gnn_W_msg",
        "L1_gnn_b_msg", "L1_gnn_W_upd", "L1_gnn_b_upd", "L1_gnn_gamma", "L1_gnn_beta"]


def kernel(**inputs):
    import numpy as _np
    import concourse.bacc as _bacc
    from concourse import mybir as _mybir
    from concourse.bass_utils import run_bass_kernel_spmd as _run

    nc = _bacc.Bacc("TRN2", target_bir_lowering=False, num_devices=1)
    arrays, args = {}, []
    for name in _INS:
        a = _np.ascontiguousarray(inputs[name])
        arrays[f"in_{name}_dram"] = a
        args.append(nc.dram_tensor(f"in_{name}_dram", a.shape, _mybir.dt.from_np(a.dtype), kind="ExternalInput").ap())
    x = inputs["x"]
    out = nc.dram_tensor("out_0_dram", tuple(x.shape), _mybir.dt.from_np(_np.dtype("float32")),
                         kind="ExternalOutput").ap()
    gnn_kernel(nc, *args, out)
    r = _run(nc, [arrays], core_ids=[0])
    return r.results[0]["out_0_dram"]
```

```python
from contextlib import ExitStack, contextmanager

import concourse.bass as bass
from concourse import mybir

ALU = mybir.AluOpType
ACT = mybir.ActivationFunctionType
F32 = mybir.dt.float32
BF16 = mybir.dt.bfloat16
I32 = mybir.dt.int32

P = 128
ROW = 2048
GROUP = 512
CH = ROW // GROUP
J = GROUP // P
NODE_BITS = 14
PAD = (1 << NODE_BITS) - 1
ONE_BIT = 1 << 30
RESET = -1e30
EPS = 1e-5
BATCH = 7
X_LEVEL = 4
UNROLL = 2


class Shapes:
    def __init__(self, nodes, edges, d, hid):
        self.nodes, self.edges, self.d, self.hid = nodes, edges, d, hid
        self.tiles = -(-nodes // P)
        self.rows = -(-edges // ROW)
        self.full_rows = edges // ROW
        self.groups = -(-edges // GROUP)
        self.chunks = hid // P
        assert d == P and self.tiles % BATCH == 0 and nodes < PAD and self.rows <= P
        assert self.chunks == 4 and self.tiles == self.rows


def reach(eng, semaphore, value):
    if not isinstance(value, int) or value > 0:
        eng.wait_ge(semaphore, value)


@contextmanager
def phase(nc):
    used = []

    def semaphore(name):
        used.append(nc.alloc_semaphore(name))
        return used[-1]

    with ExitStack() as ctx:
        yield ctx, semaphore
    nc.clear_and_free_semaphores(used)
    nc.all_engine_barrier()


class Memory:
    pass


def setup(nc, s, mem, src, dst):
    with phase(nc) as (ctx, semaphore):
        padded = semaphore("padded")
        zeroed = semaphore("zeroed")
        iotas_done = semaphore("iotas_done")
        src_landed = semaphore("src_landed")
        dst_landed = semaphore("dst_landed")
        block = ctx.enter_context(nc.Block())
        full, rest = s.full_rows, s.edges - s.full_rows * ROW
        assert rest

        @block.gpsimd
        def _(pool):
            pool.memset(mem.ident_wide[:], 0.0).then_inc(zeroed, 1)
            pool.wait_ge(zeroed, 1)
            pool.affine_select(out=mem.ident_wide[:, 1:1 + P], in_=mem.ident_wide[:, 1:1 + P],
                               compare_op=ALU.not_equal, fill=1.0, base=0, pattern=[[-1, P]],
                               channel_multiplier=1).then_inc(iotas_done, 1)
            pool.iota(mem.node_number[:], [[P, s.tiles]], base=0, channel_multiplier=1,
                      allow_small_or_imprecise_dtypes=True).then_inc(iotas_done, 1)
            pool.iota(mem.row_number[:], [[1, P]], base=0, channel_multiplier=0).then_inc(iotas_done, 1)
            pool.iota(mem.partition_number[:], [[0, 1]], base=0, channel_multiplier=1).then_inc(iotas_done, 1)

        @block.vector
        def _(dve):
            dve.memset(mem.src_rows[:], PAD).then_inc(padded, 1)
            dve.memset(mem.dst_rows[:], PAD).then_inc(padded, 1)
            dve.memset(mem.x[:, s.nodes // P * s.d:], 0.0).then_inc(padded, 1)
            dve.memset(mem.eps[:], EPS)
            dve.memset(mem.ones[:], 1.0)
            for n in range(2):
                dve.memset(mem.ends[n][:, 0:1], 0.0)
            dve.wait_ge(src_landed, 32)
            dve.tensor_copy(mem.src_given[:], mem.src_rows[:])
            dve.wait_ge(dst_landed, 32)
            dve.tensor_copy(mem.dst_given[:], mem.dst_rows[:])
            dve.wait_ge(iotas_done, 2)
            dve.tensor_scalar(mem.node_half[:], mem.node_number[:], 0.5, None, ALU.add)
            dve.tensor_copy(mem.ident_bf[:], mem.ident_wide[:, 1:1 + P])

        @block.scalar
        def _(act):
            for tile, array in mem.weights:
                act.dma_start(tile, array).then_inc(mem.weights_landed, 16)

        @block.sync
        def _(sp):
            sp.wait_ge(padded, 3)
            for edge_end, rows, landed in ((src, mem.src_rows, src_landed), (dst, mem.dst_rows, dst_landed)):
                sp.dma_start(rows[0:full, :], edge_end[0:full * ROW].rearrange("(r c) -> r c", c=ROW)
                             ).then_inc(landed, 16)
                sp.dma_start(rows[full:full + 1, 0:rest],
                             edge_end[full * ROW:s.edges].rearrange("(r c) -> r c", r=1)).then_inc(landed, 16)
            sp.wait_ge(src_landed, 32)
            sp.wait_ge(dst_landed, 32)




def make_tables(nc, s, mem, n, by_segment, gathered, index, resets, kind):
    R = s.rows
    heads_n = R * CH
    with phase(nc) as (ctx, semaphore):
        def sem(name):
            return semaphore(f"t{n}_{name}")

        column_turned, resets_made, heads_spread, diagonal_made, shifted, rows_stored, compared = (
            sem(x) for x in ("column_turned", "resets_made", "heads_spread", "diagonal_made", "shifted",
                             "rows_stored", "compared"))
        differs = ctx.enter_context(nc.sbuf_tensor(f"t{n}_differs", [P, ROW], F32))
        diagonal = ctx.enter_context(nc.sbuf_tensor(f"t{n}_diagonal", [R, R, CH], F32))
        turned = [ctx.enter_context(nc.psum_tensor(f"t{n}_turned{k}", [P, J, P], F32)) for k in range(CH)]
        head_bank = ctx.enter_context(nc.psum_tensor(f"t{n}_head_bank", [P, 512], F32))
        shift_bank = ctx.enter_context(nc.psum_tensor(f"t{n}_shift_bank", [P, 512], F32))
        block = ctx.enter_context(nc.Block())
        from_row_above = mem.ident_wide[:, 0:P]

        @block.tensor
        def _(pe):
            pe.matmul(shift_bank[:, 0:1], from_row_above, by_segment[:, ROW - 1:ROW],
                      start=True, stop=True).then_inc(shifted, 1)
            for ch in range(CH):
                for j in range(J):
                    c = ch * GROUP + j
                    turn = pe.transpose(turned[ch][:, j, 0:R], gathered[0:R, c:c + GROUP - J + 1:J],
                                        mem.ident[0:R, 0:R])
                turn.then_inc(column_turned, 1)
            pe.wait_ge(diagonal_made, 1)
            pe.matmul(head_bank[:, 0:heads_n], mem.ones[0:R, :], diagonal[:].rearrange("k r c -> k (r c)"),
                      start=True, stop=True).then_inc(heads_spread, 1)

        @block.vector
        def _(dve):
            first = by_segment[0:R, :].rearrange("r (c g) -> r c g", g=GROUP)[:, :, 0]
            dve.tensor_tensor(diagonal[:], mem.ident[0:R, 0:R].unsqueeze(2).to_broadcast([R, R, CH]),
                              first.unsqueeze(1).to_broadcast([R, R, CH]), ALU.mult).then_inc(diagonal_made, 1)
            dve.wait_ge(shifted, 1)
            to, op = (resets, ALU.is_equal) if kind == "keep" else (differs, ALU.not_equal)
            dve.tensor_tensor(to[:, 1:ROW], by_segment[:, 1:ROW], by_segment[:, 0:ROW - 1], op
                              ).then_inc(compared, 1)
            dve.tensor_tensor(to[:, 0:1], by_segment[:, 0:1], shift_bank[:, 0:1], op).then_inc(compared, 1)
            for ch in range(CH):
                dve.wait_ge(column_turned, ch + 1)
                to = index[:].rearrange("p (r c j) -> p c j r", c=CH, j=J)[:, ch, :, 0:R]
                dve.tensor_scalar(to, turned[ch][:, :, 0:R], float(s.tiles * P - 1), None, ALU.min)
            dve.wait_ge(heads_spread, 1)
            dve.tensor_copy(mem.heads[n][:], head_bank[:, 0:heads_n])
            if kind != "keep":
                dve.wait_ge(compared, 2)
                dve.tensor_scalar(resets[:], differs[:], RESET, None, ALU.mult).then_inc(resets_made, 1)

        @block.sync
        def _(sp):
            sp.dma_start(mem.segment_dram[n].rearrange("(r c) g -> r (c g)", c=CH), by_segment[0:R, :]
                         ).then_inc(rows_stored, 16)
            sp.wait_ge(rows_stored, 16)
            if kind != "keep":
                sp.wait_ge(resets_made, 1)
                sp.dma_start(mem.reset_dram.rearrange("(r c) g -> r (c g)", c=CH), resets[0:R, :]
                             ).then_inc(rows_stored, 16)
                sp.wait_ge(rows_stored, 32)


def unpack_sorted_keys(nc, s, mem):
    with phase(nc) as (ctx, semaphore):
        unpacked = semaphore("unpacked")
        field = [ctx.enter_context(nc.sbuf_tensor(f"field{n}", [P, ROW], I32)) for n in range(2)]
        block = ctx.enter_context(nc.Block())

        @block.vector
        def _(dve):
            bits = mem.sorted_keys[:].bitcast(I32)
            dve.tensor_scalar(field[0][:], bits, NODE_BITS, PAD, ALU.logical_shift_right, ALU.bitwise_and
                              ).then_inc(unpacked, 1)
            dve.tensor_scalar(field[1][:], bits, PAD, None, ALU.bitwise_and).then_inc(unpacked, 1)
            dve.wait_ge(unpacked, 1)
            dve.tensor_copy(mem.src_sorted[:], field[0][:])
            dve.wait_ge(unpacked, 2)
            dve.tensor_copy(mem.dst_sorted[:], field[1][:])


def make_search(nc, ctx, semaphore, s, mem, n, buffers):
    def sems(name):
        return [semaphore(f"search{n}_{name}{k}") for k in range(buffers)]

    def sbs(name, shape, dt=F32):
        return [ctx.enter_context(nc.sbuf_tensor(f"search{n}_{name}{k}", shape, dt)) for k in range(buffers)]

    of = Memory()
    of.mem, of.n, of.groups = mem, n, s.rows * CH
    of.heads_counted, of.doubled, of.index_made, of.fetched, of.row_counted = (
        sems("heads_counted"), sems("doubled"), sems("index_made"), sems("fetched"), sems("row_counted"))
    of.passed = semaphore(f"search{n}_passed")
    of.head_signs, of.row_signs = sbs("head_signs", [P, of.groups]), sbs("row_signs", [P, GROUP])
    of.balance, of.twice_group = sbs("balance", [P, 1]), sbs("twice_group", [P, 1])
    of.index, of.fetch = sbs("index", [P, 1], I32), sbs("fetch", [P, GROUP])
    return of


def count_heads(of, act, t, k, u):
    reach(act, of.index_made[k], u)
    act.sem_inc(of.passed, 1)
    act.activation(of.head_signs[k][:], of.mem.heads[of.n][:], ACT.Sign, scale=-1.0,
                   bias=of.mem.node_half[:, bass.ds(t, 1)], accum_out=of.balance[k][:]
                   ).then_inc(of.heads_counted[k], 1)


def fetch_group(of, pool, t, k, u):
    pool.wait_ge(of.heads_counted[k], u + 1)
    reach(pool, of.row_counted[k], u)
    pool.sem_inc(of.passed, 1)
    pool.tensor_scalar(of.twice_group[k][:], of.balance[k][:], float(2 - of.groups),
                       float(of.groups - 2), ALU.max, ALU.add).then_inc(of.doubled[k], 1)
    pool.wait_ge(of.doubled[k], u + 1)
    pool.sem_inc(of.passed, 1)
    pool.tensor_scalar(of.index[k][:], of.twice_group[k][:], 0.5, 0.0, ALU.mult, ALU.add
                       ).then_inc(of.index_made[k], 1)
    pool.tensor_copy(of.mem.twice_group[of.n][:, bass.ds(t, 1)], of.twice_group[k][:])
    pool.wait_ge(of.index_made[k], u + 1)
    pool.sem_inc(of.passed, 1)
    pool.indirect_dma_start(of.fetch[k][:], None, of.mem.segment_dram[of.n],
                            bass.IndirectOffsetOnAxis(of.index[k][:], 0)).then_inc(of.fetched[k], 16)


def count_row(of, act, t, k, u):
    act.wait_ge(of.fetched[k], (u + 1) * 16)
    act.sem_inc(of.passed, 1)
    act.activation(of.row_signs[k][:], of.fetch[k][:], ACT.Sign, scale=-1.0,
                   bias=of.mem.node_half[:, bass.ds(t, 1)],
                   accum_out=of.mem.row_balance[of.n][:, bass.ds(t, 1)]).then_inc(of.row_counted[k], 1)


def find_ends(nc, s, mem, n):
    with phase(nc) as (ctx, semaphore):
        def sem(name):
            return semaphore(f"ends{n}_{name}")

        def sb(name):
            return ctx.enter_context(nc.sbuf_tensor(f"ends{n}_{name}", [P, s.tiles], F32))

        step, ended, begun = sem("step"), sem("ended"), sem("begun")
        group_start, in_group, count, some, inverse = (
            sb(x) for x in ("group_start", "in_group", "count", "some", "inverse"))
        begin_bank = ctx.enter_context(nc.psum_tensor(f"ends{n}_begin", [P, P], F32))
        block = ctx.enter_context(nc.Block())
        ends = mem.ends[n]

        @block.tensor
        def _(pe):
            pe.wait_ge(ended, 1)
            pe.matmul(begin_bank[:, 0:s.tiles], mem.ident_wide[:, 0:P], ends[:, 1:1 + s.tiles],
                      start=True, stop=False)
            pe.matmul(begin_bank[:, 0:s.tiles], mem.ident_wide[:, P:2 * P], ends[:, 0:s.tiles],
                      start=False, stop=True).then_inc(begun, 1)

        @block.vector
        def _(dve):
            dve.tensor_scalar(group_start[:], mem.twice_group[n][:], GROUP / 2.0, None, ALU.mult).then_inc(step, 1)
            dve.tensor_scalar(in_group[:], mem.row_balance[n][:], float(GROUP), 0.5, ALU.add, ALU.mult
                              ).then_inc(step, 1)
            dve.wait_ge(step, 2)
            dve.tensor_tensor(ends[:, 1:], group_start[:], in_group[:], ALU.add).then_inc(ended, 1)
            dve.wait_ge(ended, 1)
            dve.tensor_scalar(mem.last[n][:], ends[:, 1:], -1.0, 0.0, ALU.add, ALU.max)
            dve.wait_ge(begun, 1)
            dve.tensor_tensor(count[:], ends[:, 1:], begin_bank[:, 0:s.tiles], ALU.subtract).then_inc(step, 1)
            dve.wait_ge(step, 3)
            some_to = mem.scale[0] if n == 0 else some
            dve.tensor_scalar(some_to[:], count[:], 1.0, None, ALU.min).then_inc(step, 1)
            if n == 1:
                dve.tensor_scalar(count[:], count[:], 1.0, None, ALU.max).then_inc(step, 1)
                dve.wait_ge(step, 5)
                dve.reciprocal(inverse[:], count[:]).then_inc(step, 1)
                dve.wait_ge(step, 6)
                dve.tensor_tensor(mem.scale[1][:], inverse[:], some[:], ALU.mult)




def sort_and_first_nodes(nc, s, mem):
    D = s.d
    with phase(nc) as (ctx, semaphore):
        keys_made, signs_made, compared, merged, turned, emptied = (
            semaphore(x) for x in ("keys_made", "signs_made", "compared", "merged", "turned", "emptied"))
        h_ready, h_turned, hT_ready, own_ready, own_copied, own_added = (
            semaphore(x) for x in ("h_ready", "h_turned", "hT_ready", "own_ready", "own_copied", "own_added"))
        z_made, z_copied, passed = semaphore("z_made"), semaphore("z_copied"), semaphore("first_nodes_passed")
        z_stored = [semaphore(f"z_stored{k}") for k in range(2)]
        x_landed = semaphore("x_landed")
        whole, rest_nodes = s.nodes // P, s.nodes % P
        assert rest_nodes
        measured, moments_made, rooted, inverted, shifted = (
            semaphore(f"statistics_{x}") for x in ("measured", "moments_made", "rooted", "inverted", "shifted"))
        key_banks = [ctx.enter_context(nc.psum_tensor(f"turned_keys{n}", [P, 4 * P], F32)) for n in range(2)]
        h_bank = ctx.enter_context(nc.psum_tensor("h_bank", [P, 8, P], F32))
        own_bank = ctx.enter_context(nc.psum_tensor("own_bank", [P, 8, D], F32))
        z_bank = [ctx.enter_context(nc.psum_tensor(f"z_bank{n}", [P, s.hid], F32)) for n in range(2)]

        banks = key_banks + z_bank

        def sb(name, shape, dt=F32):
            return ctx.enter_context(nc.sbuf_tensor(name, shape, dt))

        statistics, moments = sb("statistics", [P, s.tiles, 6]), sb("moments", [P, s.tiles, 2])
        root = sb("root", [P, s.tiles])
        bit, sign, flip = sb("bit", [P, 8, P], I32), sb("sign", [P, 8, P]), sb("flip", [P, 8, P])
        odd, odd_sign = sb("odd", [P, 1], I32), sb("odd_sign", [P, 1])
        h, hT, own = sb("h0", [P, BATCH, D]), sb("hT0", [P, 2, BATCH, P]), sb("own0", [P, BATCH * D])
        z = sb("z0", [P, 2, BATCH, s.hid])
        search = make_search(nc, ctx, semaphore, s, mem, 1, 2)
        block = ctx.enter_context(nc.Block())
        row_levels = ROW.bit_length() - 1
        merges_over_rows = P.bit_length() - 1
        keys = (mem.key_a, mem.key_b)
        row_steps = row_levels * (row_levels + 1) // 2
        pairs = s.tiles // (2 * BATCH)
        assert s.tiles == pairs * 2 * BATCH

        def over_batches(eng, step):
            for k in range(2):
                step(k, k, 0)
            with eng.Fori(1, pairs - 1) as u:
                for k in range(2):
                    step(u * 2 + k, k, u)
            for k in range(2):
                step(pairs * 2 - 2 + k, k, pairs - 1)

        def exists(b):
            return not isinstance(b, int) or b < 2 * pairs

        @block.tensor
        def _(pe):
            def turn_h(b):
                pe.wait_ge(h_ready, b + 1)
                reach(pe, hT_ready, b)
                for t in range(BATCH):
                    turn = pe.transpose(h_bank[:, t, :], h[:, t, :], mem.ident)
                turn.then_inc(h_turned, 1)

            def own_part(b, k):
                pe.wait_ge(hT_ready, b + 1)
                reach(pe, own_copied, b)
                for t in range(BATCH):
                    mm = pe.matmul(own_bank[:, t, :], hT[:, k, t, :], mem.w_own[:], start=True, stop=True)
                mm.then_inc(own_ready, 1)

            def nodes(b, k, u):
                if exists(b + 1):
                    turn_h(b + 1)
                for t in range(BATCH):
                    reach(pe, z_copied, b * BATCH + (t - 1))
                    pe.matmul(z_bank[(k + t) % 2][:], hT[:, k, t, :], mem.fc_w[:], start=True, stop=True
                              ).then_inc(z_made, 1)
                if exists(b + 1):
                    own_part(b + 1, 1 - k)

            turn_h(0)
            own_part(0, 0)
            over_batches(pe, nodes)

            pe.wait_ge(z_copied, s.tiles)
            steps, turns = row_steps, 0
            for m in range(1, merges_over_rows + 1):
                for following in (1 + m, 1 + row_levels):
                    for q in range(4):
                        if q % 2 == 0:
                            pe.wait_ge(merged, 4 * turns + q + 2)
                        for b in range(4):
                            c = (q * 4 + b) * P
                            turn = pe.transpose(banks[q][:, b * P:(b + 1) * P],
                                                keys[steps % 2][:, c:c + P], mem.ident)
                        turn.then_inc(turned, 1)
                    steps += following
                    turns += 1

        @block.scalar
        def _(act):
            def relu(b, t):
                column = bass.ds(b * BATCH + t, 1)
                done = act.activation(h[:, t, :], mem.x[:, bass.ds(b * (BATCH * D) + t * D, D)], ACT.Relu,
                                      bias=mem.shift[:, column], scale=mem.inverse_root[:, column])
                if t == BATCH - 1:
                    done.then_inc(h_ready, 1)

            def copy_hT(b, k):
                act.wait_ge(h_turned, b + 1)
                reach(act, z_made, (b - 1) * BATCH)
                act.copy(hT[:, k], h_bank[:, 0:BATCH, :]).then_inc(hT_ready, 1)

            def copy_own(b):
                act.wait_ge(own_ready, b + 1)
                reach(act, own_added, b)
                act.copy(own[:], own_bank[:, 0:BATCH, :].rearrange("p t d -> p (t d)")).then_inc(own_copied, 1)

            def nodes(b, k, u):
                if exists(b + 1):
                    copy_hT(b + 1, 1 - k)
                reach(act, z_stored[k], u * 16)
                for t in range(BATCH):
                    act.wait_ge(z_made, b * BATCH + (t + 1))
                    act.copy(z[:, k, t, :], z_bank[(k + t) % 2][:]).then_inc(z_copied, 1)
                    if exists(b + 2):
                        relu(b + 2, t)
                if exists(b + 1):
                    copy_own(b + 1)

            act.wait_ge(moments_made, s.tiles)
            act.activation(root[:], moments[:, :, 1], ACT.Sqrt, bias=mem.eps[:, 0:1]).then_inc(rooted, 1)
            act.wait_ge(mem.weights_landed, 16 * len(mem.weights))
            act.wait_ge(shifted, 1)
            act.sem_inc(passed, 1)
            for t in range(BATCH):
                relu(0, t)
            copy_hT(0, 0)
            for t in range(BATCH):
                relu(1, t)
            copy_own(0)
            over_batches(act, nodes)
            for k in range(2):
                count_heads(search, act, k, k, 0)
            with act.Fori(1, s.tiles // 2) as u:
                for k in range(2):
                    count_heads(search, act, u * 2 + k, k, u)
                    count_row(search, act, u * 2 + (k - 2), k, u - 1)
            for k in range(2):
                count_row(search, act, s.tiles - 2 + k, k, s.tiles // 2 - 1)

        @block.gpsimd
        def _(pool):
            def nodes(b, k, u):
                pool.wait_ge(own_copied, b + 1)
                pool.sem_inc(passed, 1)
                x = mem.x[:, bass.ds(b * (BATCH * D), BATCH * D)]
                pool.tensor_tensor(x, x, own[:], ALU.add).then_inc(own_added, 1)

            over_batches(pool, nodes)
            for k in range(2):
                fetch_group(search, pool, k, k, 0)
            with pool.Fori(1, s.tiles // 2) as u:
                for k in range(2):
                    fetch_group(search, pool, u * 2 + k, k, u)

        @block.sync
        def _(sp):
            sp.dma_start(mem.x[:, 0:whole * s.d].rearrange("p (t d) -> p t d", d=s.d),
                         mem.x_dram[0:whole * P, :].rearrange("(t p) d -> p t d", p=P)).then_inc(x_landed, 16)
            sp.dma_start(mem.x[0:rest_nodes, whole * s.d:], mem.x_dram[whole * P:s.nodes, :]
                         ).then_inc(x_landed, 16)

            def nodes(b, k, u):
                sp.wait_ge(z_copied, (b + 1) * BATCH)
                sp.dma_start(mem.z_dram[bass.ds(b * (BATCH * P), BATCH * P), :].rearrange("(t p) f -> p t f", p=P),
                             z[:, k]).then_inc(z_stored[k], 16)

            over_batches(sp, nodes)
            for k in range(2):
                sp.wait_ge(z_stored[k], pairs * 16)

        @block.vector
        def _(dve):
            n = 0
            turns = 0

            def halves(a, stride, mirrored=False):
                v = a[:].rearrange("p (g two j) -> p g two j", two=2, j=stride)
                return v[:, :, 0, :], v[:, :, 1, ::-1] if mirrored else v[:, :, 1, :]

            def compare(step, stride, mirrored=False, last=False):
                nonlocal n
                low, high = halves(keys[step % 2], stride, mirrored)
                low_to, high_to = halves(keys[(step + 1) % 2], stride, mirrored)
                if last:
                    g = low.shape[1] // 2
                    for part in (slice(0, g), slice(g, 2 * g)):
                        dve.tensor_tensor(low_to[:, part], low[:, part], high[:, part], ALU.min).then_inc(merged, 1)
                        dve.tensor_tensor(high_to[:, part], low[:, part], high[:, part], ALU.max).then_inc(merged, 1)
                    return
                dve.tensor_tensor(low_to, low, high, ALU.min).then_inc(compared, 1)
                dve.tensor_tensor(high_to, low, high, ALU.max).then_inc(compared, 1)
                n += 2
                dve.wait_ge(compared, n)

            def measure_rows_of_x():
                dve.wait_ge(x_landed, 32)
                dve.sem_inc(passed, 1)
                for t in range(s.tiles):
                    dve.bn_stats(statistics[:, t, :], mem.x[:, t * D:(t + 1) * D]).then_inc(measured, 1)
                dve.wait_ge(measured, s.tiles)
                for t in range(s.tiles):
                    dve.bn_aggr(moments[:, t, :], statistics[:, t, :]).then_inc(moments_made, 1)

            def make_scale_and_shift():
                dve.wait_ge(rooted, 1)
                dve.reciprocal(mem.inverse_root[:], root[:]).then_inc(inverted, 1)
                dve.wait_ge(inverted, 1)
                dve.scalar_tensor_tensor(mem.shift[:], moments[:, :, 0], -1.0, mem.inverse_root[:],
                                         ALU.mult, ALU.mult).then_inc(shifted, 1)

            for m in range(0, 8):
                dve.tensor_scalar(bit[:, m, :], mem.row_number[:], m, 1, ALU.logical_shift_right, ALU.bitwise_and
                                  ).then_inc(signs_made, 1)
            for m in range(0, 8):
                dve.wait_ge(signs_made, 8 + m)
                dve.tensor_scalar(sign[:, m, :], bit[:, m, :], -2.0, 1.0, ALU.mult, ALU.add
                                  ).then_inc(signs_made, 1)
            dve.wait_ge(signs_made, 16)
            dve.tensor_tensor(flip[:, 1:8, :], sign[:, 1:8, :], sign[:, 0:7, :], ALU.mult).then_inc(signs_made, 1)
            dve.tensor_scalar(odd[:], mem.partition_number[:], 1, None, ALU.bitwise_and).then_inc(signs_made, 1)
            dve.wait_ge(signs_made, 18)
            dve.tensor_scalar(odd_sign[:], odd[:], -2.0, 1.0, ALU.mult, ALU.add).then_inc(signs_made, 1)

            key_bits = mem.key_b[:].bitcast(I32)
            dve.tensor_scalar(key_bits, mem.src_rows[:], NODE_BITS, ONE_BIT, ALU.logical_shift_left,
                              ALU.bitwise_or).then_inc(keys_made, 1)
            dve.wait_ge(keys_made, 1)
            dve.tensor_tensor(key_bits, key_bits, mem.dst_rows[:], ALU.bitwise_or).then_inc(keys_made, 1)
            dve.wait_ge(keys_made, 2)
            dve.wait_ge(signs_made, 19)
            dve.tensor_scalar(mem.key_a[:], mem.key_b[:], odd_sign[:, 0:1], None, ALU.mult).then_inc(keys_made, 1)
            dve.wait_ge(keys_made, 3)

            step = 0
            for level in range(1, row_levels + 1):
                if level == X_LEVEL:
                    measure_rows_of_x()
                compare(step, 1 << (level - 1), mirrored=True)
                step += 1
                if level == X_LEVEL:
                    make_scale_and_shift()
                for j in range(level - 2, -1, -1):
                    compare(step, 1 << j, last=(level == row_levels and j == 0))
                    step += 1
            for m in range(1, merges_over_rows + 1):
                for strides, signed in ((m, True), (row_levels, False)):
                    for q in range(4):
                        dve.wait_ge(turned, 4 * turns + q + 1)
                        to = keys[(step + 1) % 2][:, q * GROUP:(q + 1) * GROUP]
                        if signed:
                            dve.tensor_tensor(to.rearrange("p (b r) -> p b r", r=P),
                                              banks[q][:].rearrange("p (b r) -> p b r", r=P),
                                              flip[:, m:m + 1, :].to_broadcast([P, 4, P]),
                                              ALU.mult).then_inc(emptied, 1)
                        else:
                            dve.tensor_copy(to, banks[q][:]).then_inc(emptied, 1)
                    turns += 1
                    dve.wait_ge(emptied, 4 * turns)
                    step += 1
                    for j in range(strides - 1, -1, -1):
                        compare(step, 1 << j, last=j == 0)
                        step += 1
            assert keys[step % 2] is mem.sorted_keys


def before(r, ch, n):
    return (r, ch - n) if ch >= n else (r - 1, ch + CH - n)


def of_two(r, ch):
    return r * (CH // 2) + ch // 2


def over_groups(eng, step, rows, tail):
    def row(r, chunks):
        for ch in chunks:
            def lagged(f, n):
                if not isinstance(r, int) or r > 0 or ch >= n:
                    f(*before(r, ch, n))
            step(r, ch, lagged)
    row(0, range(CH))
    assert (rows - 1) % UNROLL == 0
    with eng.Fori(0, (rows - 1) // UNROLL) as i:
        for k in range(UNROLL):
            row(i * UNROLL + (k + 1), range(CH))
    row(rows, range(tail))


def is_group(r, ch, *those):
    return isinstance(r, int) and (r, ch) in those


def gather_group(pool, table, index, column, staged, rows, copied, copies, begun, landed):
    pool.tensor_copy(staged, index[:, bass.ds(column, J)]).then_inc(copied, 1)
    pool.wait_ge(copied, copies)
    pool.sem_inc(begun, 1)
    for j in range(J):
        pool.indirect_dma_start(rows[:, j, :], None, table, bass.IndirectOffsetOnAxis(staged[:, j:j + 1], 0)
                                ).then_inc(landed, 16)


def result_rows(dram, g):
    return dram[bass.ds(g * GROUP, GROUP), :].rearrange("(p j) d -> p (j d)", j=J)


def edges_of_layer0(nc, s, mem):
    D, C, H = s.d, s.chunks, s.hid
    with phase(nc) as (ctx, semaphore):
        def sems(name, n):
            return [semaphore(f"e0_{name}{k}") for k in range(n)]

        def sb(name, shape, dt=F32):
            return ctx.enter_context(nc.sbuf_tensor("e0_" + name, shape, dt))

        copied, begun, relu_done = sems("copied", 1)[0], sems("begun", 1)[0], sems("relu_done", 1)[0]
        landed = sems("landed", CH)
        mask_landed = sems("mask_landed", CH)
        z_ready, scanned = sems("z_ready", C), sems("scanned", C)
        y_ready, y_copied, stored = sems("y_ready", 1)[0], sems("y_copied", 2), sems("stored", 2)

        staged = sb("staged", [P, CH, J], I32)
        rows = [sb(f"rows{k}", [P, J, H]) for k in range(CH)]
        mask = sb("mask", [P, CH, GROUP], BF16)
        best = sb("best", [P, 2, C, GROUP])
        agg = sb("agg", [P, 2, C, GROUP])
        y = sb("y", [P, 2, J * D])
        z = [ctx.enter_context(nc.psum_tensor(f"e0_z{c}", [P, GROUP], F32)) for c in range(C)]
        y_bank = [ctx.enter_context(nc.psum_tensor(f"e0_y_bank{k}", [P, J * D], F32)) for k in range(2)]
        search = make_search(nc, ctx, semaphore, s, mem, 0, 1)
        block = ctx.enter_context(nc.Block())

        def over_all(eng, step):
            over_groups(eng, step, s.rows - 1, CH)

        @block.gpsimd
        def _(pool):
            def step(r, ch, lagged):
                if not (isinstance(r, int) and r == 0):
                    pool.wait_ge(z_ready[C - 1], (r - 1) * CH + (ch + 1))
                gather_group(pool, mem.z_dram, mem.index[0], r * (CH * J) + ch * J, staged[:, ch, :],
                             rows[ch], copied, r * CH + (ch + 1), begun, landed[ch])
                if ch == 1 and not (isinstance(r, int) and r == 0):
                    fetch_group(search, pool, r - 1, 0, r - 1)
            over_all(pool, step)
            fetch_group(search, pool, s.rows - 1, 0, s.rows - 1)

        @block.tensor
        def _(pe):
            def turn(r, ch, c):
                if c == 0:
                    pe.wait_ge(landed[ch], (r + 1) * (16 * J))
                reach(pe, scanned[c], r * CH + ch)
                for j in range(J):
                    t = pe.transpose(z[c][:, j::J], rows[ch][:, j, c * P:(c + 1) * P], mem.ident)
                t.then_inc(z_ready[c], 1)

            def project(r, ch, j):
                k = ch % 2
                if j == 0:
                    pe.wait_ge(relu_done, (r * CH + (ch + 1)) * C)
                    reach(pe, y_copied[k], of_two(r, ch))
                for c in range(C):
                    mm = pe.matmul(y_bank[k][:, j * D:(j + 1) * D], agg[:, k, c, j::J], mem.w_agg[:, c, :],
                                   start=c == 0, stop=c == C - 1)
                if j == J - 1:
                    mm.then_inc(y_ready, 1)

            def step(r, ch, lagged):
                for c in range(C):
                    turn(r, ch, c)
                    lagged(lambda r2, ch2: project(r2, ch2, c), 2)
            over_all(pe, step)
            for n in (2, 1):
                for j in range(J):
                    project(*before(s.rows, 0, n), j)

        @block.scalar
        def _(act):
            def rectify(r, ch):
                if not is_group(r, ch, (0, 0), (0, 1)):
                    r2, ch2 = before(r, ch, 2)
                    act.wait_ge(y_ready, r2 * CH + (ch2 + 1))
                for c in range(C):
                    act.wait_ge(scanned[c], r * CH + (ch + 1))
                    act.activation(agg[:, ch % 2, c, :], best[:, ch % 2, c, :], ACT.Relu,
                                   bias=mem.fc_b[:, c:c + 1]).then_inc(relu_done, 1)

            def copy_y(r, ch):
                k = ch % 2
                act.wait_ge(y_ready, r * CH + (ch + 1))
                reach(act, stored[k], of_two(r, ch) * 16)
                act.copy(y[:, k, :], y_bank[k][:]).then_inc(y_copied[k], 1)

            def step(r, ch, lagged):
                lagged(copy_y, 3)
                lagged(rectify, 1)
                if ch == 0:
                    count_heads(search, act, r, 0, r)
                elif ch == 2 and not (isinstance(r, int) and r == 0):
                    count_row(search, act, r - 1, 0, r - 1)
            over_all(act, step)
            rectify(*before(s.rows, 0, 1))
            for n in (3, 2, 1):
                copy_y(*before(s.rows, 0, n))
            count_row(search, act, s.rows - 1, 0, s.rows - 1)

        @block.vector
        def _(dve):
            def step(r, ch, lagged):
                k = ch % 2
                dve.wait_ge(mask_landed[ch], (r + 1) * 16)
                for c in range(C):
                    dve.wait_ge(z_ready[c], r * CH + (ch + 1))
                    if is_group(r, ch, (0, 0)):
                        state = RESET
                    else:
                        dve.wait_ge(scanned[c], r * CH + ch)
                        state = best[:, 1 - k, c, GROUP - 1:GROUP]
                    if not is_group(r, ch, (0, 0), (0, 1)):
                        r2, ch2 = before(r, ch, 2)
                        dve.wait_ge(relu_done, (r2 * CH + ch2) * C + (c + 1))
                    dve.tensor_tensor_scan(best[:, k, c, :], mask[:, ch, :], z[c][:], state,
                                           ALU.add, ALU.max).then_inc(scanned[c], 1)
            over_all(dve, step)

        @block.sync
        def _(sp):
            def load_mask(r, ch):
                if not (isinstance(r, int) and r == 0):
                    sp.wait_ge(scanned[C - 1], (r - 1) * CH + (ch + 1))
                sp.dma_start(mask[:, ch, :], mem.reset_dram[bass.ds(r * CH + ch, 1), :].to_broadcast([P, GROUP])
                             ).then_inc(mask_landed[ch], 16)

            def store(r, ch):
                sp.wait_ge(y_copied[ch % 2], of_two(r, ch) + 1)
                sp.dma_start(result_rows(mem.result_dram, r * CH + ch), y[:, ch % 2, :]
                             ).then_inc(stored[ch % 2], 16)

            def step(r, ch, lagged):
                load_mask(r, ch)
                lagged(store, 4)
            over_all(sp, step)
            for n in (4, 3, 2, 1):
                store(*before(s.rows, 0, n))
            for k in range(2):
                sp.wait_ge(stored[k], s.rows * (CH // 2) * 16)


def edges_of_layer1(nc, s, mem, edge_attr):
    D = s.d
    with phase(nc) as (ctx, semaphore):
        def sems(name, n=CH):
            return [semaphore(f"e1_{name}{k}") for k in range(n)]

        def sb(name, shape, dt=F32):
            return ctx.enter_context(nc.sbuf_tensor("e1_" + name, shape, dt))

        staged_ready, begun = sems("staged_ready"), semaphore("e1_begun")
        landed, attr_landed, attr_turned, z_ready = (
            sems("landed"), sems("attr_landed"), sems("attr_turned"), sems("z_ready"))
        attrT_ready, mask_ready, relu_done = sems("attrT_ready", 2), sems("mask_ready", 2), sems("relu_done", 2)
        mask_spread = sems("mask_spread", 1)[0]
        scanned, back_turned, sums_ready, stored = (
            sems("scanned"), sems("back_turned"), sems("sums_ready"), sems("stored"))
        tail_cleared, passed = semaphore("e1_tail_cleared"), semaphore("e1_passed")

        staged = sb("staged", [P, CH, J], I32)
        rows = sb("rows", [P, CH, J, D])
        attr = sb("attr", [P, CH, J * D])
        attrT = sb("attrT", [P, 2, GROUP])
        mask = sb("mask", [P, 2, GROUP], BF16)
        message = sb("message", [P, 2, GROUP])
        total = sb("total", [P, CH, GROUP])
        sums = sb("sums", [P, CH, J * D])
        turned = [ctx.enter_context(nc.psum_tensor(f"e1_turned{k}", [P, GROUP], F32)) for k in range(2)]
        mask_bank = ctx.enter_context(nc.psum_tensor("e1_mask_bank", [P, GROUP], F32))
        z = [ctx.enter_context(nc.psum_tensor(f"e1_z{k}", [P, GROUP], F32)) for k in range(2)]
        back = [ctx.enter_context(nc.psum_tensor(f"e1_back{k}", [P, J * D], F32)) for k in range(2)]
        block = ctx.enter_context(nc.Block())
        tail = s.groups - s.full_rows * CH
        tail_rows = (s.edges % GROUP) // J
        assert tail_rows * J == s.edges % GROUP and 0 < tail_rows and 0 < tail < CH
        last_row = s.full_rows

        def over_rows(eng, step):
            over_groups(eng, step, last_row, tail)

        @block.gpsimd
        def _(pool):
            def step(r, ch, lagged):
                pool.wait_ge(staged_ready[ch], r + 1)
                pool.sem_inc(begun, 1)
                for j in range(J):
                    pool.indirect_dma_start(rows[:, ch, j, :], None, mem.message_dram,
                                            bass.IndirectOffsetOnAxis(staged[:, ch, j:j + 1], 0)
                                            ).then_inc(landed[ch], 16)
            over_rows(pool, step)

        @block.sync
        def _(sp):
            def step(r, ch, lagged):
                if isinstance(r, int) and (r, ch) == (last_row, tail - 1):
                    sp.wait_ge(tail_cleared, 1)
                    sp.dma_start(attr[0:tail_rows, ch, :],
                                 edge_attr[(r * CH + ch) * GROUP:s.edges, :].rearrange("(p j) d -> p (j d)", j=J)
                                 ).then_inc(attr_landed[ch], 16)
                else:
                    reach(sp, attr_turned[ch], r)
                    sp.dma_start(attr[:, ch, :], result_rows(edge_attr, r * CH + ch)
                                 ).then_inc(attr_landed[ch], 16)
            over_rows(sp, step)
            for ch in range(CH):
                sp.wait_ge(stored[ch], (last_row + (ch < tail)) * 16)

        @block.tensor
        def _(pe):
            def turn(r, ch):
                k = ch % 2
                pe.wait_ge(attr_landed[ch], (r + 1) * 16)
                reach(pe, attrT_ready[k], of_two(r, ch))
                for j in range(J):
                    t = pe.transpose(turned[k][:, j::J], attr[:, ch, j * D:(j + 1) * D], mem.ident)
                t.then_inc(attr_turned[ch], 1)
                last = before(r, ch, 1) if not (isinstance(r, int) and r == 0 and ch == 0) else None
                if last:
                    pe.wait_ge(mask_ready[last[1] % 2], of_two(*last) + 1)
                pe.matmul(mask_bank[:], mem.ident_bf[:, bass.ds(r, 1)].to_broadcast([P, P]),
                          mem.resets[1][:, ch * GROUP:(ch + 1) * GROUP], start=True, stop=True
                          ).then_inc(mask_spread, 1)

            def combine(r, ch):
                k = ch % 2
                pe.wait_ge(attrT_ready[k], of_two(r, ch) + 1)
                pe.wait_ge(landed[ch], (r + 1) * (16 * J))
                reach(pe, relu_done[k], of_two(r, ch))
                pe.matmul(z[k][:], mem.wm_attr[:], attrT[:, k, :], start=True, stop=False)
                for j in range(J):
                    mm = pe.matmul(z[k][:, j::J], rows[:, ch, j, :], mem.ident, start=False, stop=j == J - 1)
                mm.then_inc(z_ready[ch], 1)

            def turn_back(r, ch):
                pe.wait_ge(scanned[ch], r + 1)
                if not (isinstance(r, int) and r == 0 and ch < 2):
                    r2, ch2 = before(r, ch, 2)
                    pe.wait_ge(sums_ready[ch2], r2 + 1)
                for j in range(J):
                    t = pe.transpose(back[ch % 2][:, j * D:(j + 1) * D], total[:, ch, j::J], mem.ident)
                t.then_inc(back_turned[ch], 1)

            def step(r, ch, lagged):
                turn(r, ch)
                lagged(combine, 1)
                lagged(turn_back, 3)
            over_rows(pe, step)
            combine(last_row, tail - 1)
            for n in (3, 2, 1):
                turn_back(*before(last_row, tail, n))

        @block.scalar
        def _(act):
            def spread(r, ch):
                k = ch % 2
                act.wait_ge(attr_turned[ch], r + 1)
                if not (isinstance(r, int) and r == 0 and ch < 2):
                    r2, ch2 = before(r, ch, 2)
                    act.wait_ge(scanned[ch2], r2 + 1)
                act.copy(attrT[:, k, :], turned[k][:]).then_inc(attrT_ready[k], 1)
                act.wait_ge(mask_spread, r * CH + (ch + 1))
                act.copy(mask[:, k, :], mask_bank[:]).then_inc(mask_ready[k], 1)

            def rectify(r, ch):
                act.wait_ge(z_ready[ch], r + 1)
                act.activation(message[:, ch % 2, :], z[ch % 2][:], ACT.Relu, bias=mem.b_msg[:, 0:1]
                               ).then_inc(relu_done[ch % 2], 1)

            def store(r, ch):
                act.wait_ge(sums_ready[ch], r + 1)
                act.dma_start(result_rows(mem.result_dram, r * CH + ch), sums[:, ch, :]).then_inc(stored[ch], 16)

            def step(r, ch, lagged):
                spread(r, ch)
                lagged(rectify, 1)
                lagged(store, 4)
            over_rows(act, step)
            rectify(last_row, tail - 1)
            for n in (4, 3, 2, 1):
                store(*before(last_row, tail, n))

        @block.vector
        def _(dve):
            def scan(r, ch):
                k = ch % 2
                dve.wait_ge(mask_ready[k], of_two(r, ch) + 1)
                dve.wait_ge(relu_done[k], of_two(r, ch) + 1)
                reach(dve, back_turned[ch], r)
                if isinstance(r, int) and (r, ch) == (0, 0):
                    state = 0.0
                else:
                    r1, ch1 = before(r, ch, 1)
                    dve.wait_ge(scanned[ch1], r1 + 1)
                    state = total[:, ch1, GROUP - 1:GROUP]
                dve.tensor_tensor_scan(total[:, ch, :], mask[:, k, :], message[:, k, :], state,
                                       ALU.mult, ALU.add).then_inc(scanned[ch], 1)

            def empty(r, ch):
                dve.wait_ge(back_turned[ch], r + 1)
                reach(dve, stored[ch], r * 16)
                dve.tensor_copy(sums[:, ch, :], back[ch % 2][:]).then_inc(sums_ready[ch], 1)

            def stage_indices(r, ch):
                reach(dve, z_ready[ch], r)
                dve.sem_inc(passed, 1)
                dve.tensor_copy(staged[:, ch, :], mem.index[1][:, bass.ds(r * (CH * J) + ch * J, J)]
                                ).then_inc(staged_ready[ch], 1)

            for ch in range(CH):
                stage_indices(0, ch)

            def step(r, ch, lagged):
                if not isinstance(r, int) or r + 1 < last_row or (r + 1 == last_row and ch < tail):
                    stage_indices(r + 1, ch)
                if isinstance(r, int) and (r, ch) == (last_row, 0):
                    dve.wait_ge(attr_turned[tail - 1], last_row)
                    dve.memset(attr[:, tail - 1, :], 0.0).then_inc(tail_cleared, 1)
                scan(r, ch)
                lagged(empty, 3)
            over_rows(dve, step)
            for n in (3, 2, 1):
                empty(*before(last_row, tail, n))




def over_batches(eng, s, step):
    pairs = s.tiles // (2 * BATCH)

    def one(b, k, u):
        def lagged(f):
            if not isinstance(b, int) or b > 0:
                f(b - 1, 1 - k, u if k else u - 1)
        step(b, k, u, lagged)
    for k in range(2):
        one(k, k, 0)
    with eng.Fori(1, pairs) as u:
        for k in range(2):
            one(u * 2 + k, k, u)


def last_batch(s):
    batches = s.tiles // BATCH
    return batches - 1, 1, batches // 2 - 1


def make_norm(nc, ctx, semaphore, mem, name):
    norm = Memory()
    norm.eps = mem.eps
    norm.measured, norm.moments_made, norm.rooted, norm.inverted, norm.shifted, norm.passed = (
        semaphore(f"{name}_{x}") for x in ("measured", "moments_made", "rooted", "inverted", "shifted", "passed"))
    norm.statistics = ctx.enter_context(nc.sbuf_tensor(f"{name}_statistics", [P, BATCH, 6], F32))
    norm.moments = ctx.enter_context(nc.sbuf_tensor(f"{name}_moments", [P, BATCH, 2], F32))
    norm.root = ctx.enter_context(nc.sbuf_tensor(f"{name}_root", [P, BATCH], F32))
    norm.inverse = ctx.enter_context(nc.sbuf_tensor(f"{name}_inverse", [P, BATCH], F32))
    norm.shift = ctx.enter_context(nc.sbuf_tensor(f"{name}_shift", [P, BATCH], F32))
    return norm


def measure_rows(norm, dve, b, tile):
    dve.sem_inc(norm.passed, 1)
    for t in range(BATCH):
        dve.bn_stats(norm.statistics[:, t, :], tile(t)).then_inc(norm.measured, 1)
    dve.wait_ge(norm.measured, (b + 1) * BATCH)
    dve.sem_inc(norm.passed, 1)
    for t in range(BATCH):
        dve.bn_aggr(norm.moments[:, t, :], norm.statistics[:, t, :]).then_inc(norm.moments_made, 1)


def take_roots(norm, act, b):
    act.wait_ge(norm.moments_made, (b + 1) * BATCH)
    act.activation(norm.root[:], norm.moments[:, :, 1], ACT.Sqrt, bias=norm.eps[:, 0:1]).then_inc(norm.rooted, 1)


def make_scale_and_shift(norm, dve, b):
    dve.wait_ge(norm.rooted, b + 1)
    dve.reciprocal(norm.inverse[:], norm.root[:]).then_inc(norm.inverted, 1)
    dve.wait_ge(norm.inverted, b + 1)
    dve.scalar_tensor_tensor(norm.shift[:], norm.moments[:, :, 0], -1.0, norm.inverse[:], ALU.mult, ALU.mult
                             ).then_inc(norm.shifted, 1)


def node_rows(dram, b):
    return dram[bass.ds(b * (BATCH * P), BATCH * P), :].rearrange("(t p) d -> p t d", p=P)


def gather_last_rows(pool, s, last, table, staged, rows, copied, begun, landed, used, b, k, u):
    reach(pool, used[k], u)
    pool.tensor_copy(staged[:, k, :], last[:, bass.ds(b * BATCH, BATCH)]).then_inc(copied, 1)
    pool.wait_ge(copied, b + 1)
    pool.sem_inc(begun, 1)
    for t in range(BATCH):
        pool.indirect_dma_start(rows[:, k, t, :], None, table,
                                bass.IndirectOffsetOnAxis(staged[:, k, t:t + 1], 0)).then_inc(landed[k], 16)


def nodes_between_layers(nc, s, mem):
    D = s.d
    with phase(nc) as (ctx, semaphore):
        norm = make_norm(nc, ctx, semaphore, mem, "norm_b")

        def sem(name):
            return semaphore("between_" + name)

        def sb(name, shape, dt=F32):
            return ctx.enter_context(nc.sbuf_tensor("between_" + name, shape, dt))

        copied, begun, passed, h_ready, h_turned, hT_ready, h_beta_made = (
            sem(x) for x in ("copied", "begun", "passed", "h_ready", "h_turned", "hT_ready", "h_beta_made"))
        product_ready, message_ready, own_product_ready, own_ready = (
            sem(x) for x in ("product_ready", "message_ready", "own_product_ready", "own_ready"))
        landed, used, message_stored, own_stored = (
            [sem(f"{x}{k}") for k in range(2)] for x in ("landed", "used", "message_stored", "own_stored"))
        staged = sb("staged", [P, 2, BATCH], I32)
        rows, h, message = sb("rows", [P, 2, BATCH, D]), sb("h", [P, 2, BATCH, D]), sb("message", [P, 2, BATCH, D])
        hT, own = sb("hT", [P, 2, BATCH * P]), sb("own", [P, 2, BATCH, D])
        turned = ctx.enter_context(nc.psum_tensor("between_turned", [P, 8 * P], F32))
        product, own_product = (
            ctx.enter_context(nc.psum_tensor(f"between_{x}", [P, 8, D], F32)) for x in ("product", "own_product"))
        block = ctx.enter_context(nc.Block())

        @block.gpsimd
        def _(pool):
            over_batches(pool, s, lambda b, k, u, lagged: gather_last_rows(
                pool, s, mem.last[0], mem.result_dram, staged, rows, copied, begun, landed, used, b, k, u))

        @block.vector
        def _(dve):
            def use_h(b, k, u):
                dve.wait_ge(h_ready, (b + 1) * BATCH)
                dve.sem_inc(norm.passed, 1)
                dve.tensor_tensor(mem.h_beta[:, bass.ds(b * (BATCH * D), BATCH * D)].rearrange(
                    "p (t d) -> p t d", d=D), h[:, k], mem.beta[:].unsqueeze(1).to_broadcast([P, BATCH, D]), ALU.add
                    ).then_inc(h_beta_made, 1)
                dve.wait_ge(own_product_ready, b + 1)
                reach(dve, own_stored[k], u * 16)
                dve.tensor_tensor(own[:, k], own_product[:, 0:BATCH, :],
                                  mem.b_upd[:].unsqueeze(1).to_broadcast([P, BATCH, D]), ALU.add
                                  ).then_inc(own_ready, 1)

            def step(b, k, u, lagged):
                def x_tile(t):
                    return mem.x[:, bass.ds(b * (BATCH * D) + t * D, D)]
                dve.wait_ge(landed[k], (u + 1) * (16 * BATCH))
                dve.sem_inc(norm.passed, 1)
                for t in range(BATCH):
                    add = dve.scalar_tensor_tensor(x_tile(t), rows[:, k, t, :],
                                                   mem.scale[0][:, bass.ds(b * BATCH + t, 1)],
                                                   x_tile(t), ALU.mult, ALU.add)
                add.then_inc(used[k], 1)
                dve.wait_ge(used[k], u + 1)
                measure_rows(norm, dve, b, x_tile)
                make_scale_and_shift(norm, dve, b)
                lagged(use_h)
            over_batches(dve, s, step)
            use_h(*last_batch(s))

        @block.scalar
        def _(act):
            def copy_message(b, k, u):
                act.wait_ge(product_ready, b + 1)
                reach(act, message_stored[k], u * 16)
                act.copy(message[:, k], product[:, 0:BATCH, :]).then_inc(message_ready, 1)

            def step(b, k, u, lagged):
                take_roots(norm, act, b)
                if not isinstance(b, int) or b >= 2:
                    act.wait_ge(h_beta_made, b - 1)
                act.wait_ge(norm.shifted, b + 1)
                act.sem_inc(passed, 1)
                for t in range(BATCH):
                    act.activation(h[:, k, t, :], mem.x[:, bass.ds(b * (BATCH * D) + t * D, D)], ACT.Relu,
                                   bias=norm.shift[:, t:t + 1], scale=norm.inverse[:, t:t + 1]).then_inc(h_ready, 1)
                lagged(copy_message)
                act.wait_ge(h_turned, b + 1)
                if not isinstance(b, int) or b >= 2:
                    act.wait_ge(own_product_ready, b - 1)
                act.copy(hT[:, k, :], turned[:, 0:BATCH * P]).then_inc(hT_ready, 1)
            over_batches(act, s, step)
            copy_message(*last_batch(s))

        @block.tensor
        def _(pe):
            def step(b, k, u, lagged):
                pe.wait_ge(h_ready, (b + 1) * BATCH)
                reach(pe, hT_ready, b)
                for t in range(BATCH):
                    turn = pe.transpose(turned[:, t * P:(t + 1) * P], h[:, k, t, :], mem.ident)
                turn.then_inc(h_turned, 1)
                pe.wait_ge(hT_ready, b + 1)
                for bank, weight, emptied, made in ((product, mem.wm_own, message_ready, product_ready),
                                                    (own_product, mem.wu_own, own_ready, own_product_ready)):
                    reach(pe, emptied, b)
                    for t in range(BATCH):
                        mm = pe.matmul(bank[:, t, :], hT[:, k, t * P:(t + 1) * P], weight[:], start=True, stop=True)
                    mm.then_inc(made, 1)
            over_batches(pe, s, step)

        @block.sync
        def _(sp):
            def step(b, k, u, lagged):
                sp.wait_ge(message_ready, b + 1)
                sp.dma_start(node_rows(mem.message_dram, b), message[:, k]).then_inc(message_stored[k], 16)
                sp.wait_ge(own_ready, b + 1)
                sp.dma_start(mem.own_dram[bass.ds(b * P, P), :], own[:, k].rearrange("p t d -> p (t d)")
                             ).then_inc(own_stored[k], 16)
            over_batches(sp, s, step)
            for k in range(2):
                sp.wait_ge(own_stored[k], s.tiles // (2 * BATCH) * 16)
                sp.wait_ge(message_stored[k], s.tiles // (2 * BATCH) * 16)


def nodes_after_layer1(nc, s, mem, out):
    D = s.d
    with phase(nc) as (ctx, semaphore):
        norm = make_norm(nc, ctx, semaphore, mem, "norm_u")

        def sem(name):
            return semaphore("after_" + name)

        def sb(name, shape, dt=F32):
            return ctx.enter_context(nc.sbuf_tensor("after_" + name, shape, dt))

        copied, begun, rowsT_ready, product_ready, combined, normalised, weighed, summed, finished, passed = (
            sem(x) for x in ("copied", "begun", "rowsT_ready", "product_ready", "combined", "normalised",
                             "weighed", "summed", "finished", "passed"))
        landed, turned_rows, own_landed, stored = (
            [sem(f"{x}{k}") for k in range(2)] for x in ("landed", "turned_rows", "own_landed", "stored"))
        staged = sb("staged", [P, 2, BATCH], I32)
        rows, rowsT, own, update, normal, result = (
            sb(x, [P, 2, BATCH, D]) for x in ("rows", "rowsT", "own", "update", "normal", "result"))
        turned = ctx.enter_context(nc.psum_tensor("after_turned", [P, 8, P], F32))
        product = [ctx.enter_context(nc.psum_tensor(f"after_product{k}", [P, 8, D], F32)) for k in range(2)]
        block = ctx.enter_context(nc.Block())
        batches = s.tiles // BATCH

        @block.gpsimd
        def _(pool):
            over_batches(pool, s, lambda b, k, u, lagged: gather_last_rows(
                pool, s, mem.last[1], mem.result_dram, staged, rows, copied, begun, landed, turned_rows, b, k, u))

        @block.tensor
        def _(pe):
            def step(b, k, u, lagged):
                pe.wait_ge(landed[k], (u + 1) * (16 * BATCH))
                reach(pe, rowsT_ready, b)
                for t in range(BATCH):
                    turn = pe.transpose(turned[:, t, :], rows[:, k, t, :], mem.ident)
                turn.then_inc(turned_rows[k], 1)
                if not isinstance(b, int) or b >= 2:
                    pe.wait_ge(combined, (b - 1) * BATCH)
                pe.wait_ge(rowsT_ready, b + 1)
                for t in range(BATCH):
                    mm = pe.matmul(product[k][:, t, :], rowsT[:, k, t, :], mem.wu_mean[:], start=True, stop=True)
                mm.then_inc(product_ready, 1)
            over_batches(pe, s, step)

        @block.scalar
        def _(act):
            def normalise(b, k, u):
                take_roots(norm, act, b)
                act.wait_ge(norm.shifted, b + 1)
                if not isinstance(b, int) or b >= 2:
                    act.wait_ge(finished, b - 1)
                act.sem_inc(passed, 1)
                for t in range(BATCH):
                    act.activation(normal[:, k, t, :], update[:, k, t, :], ACT.Identity,
                                   bias=norm.shift[:, t:t + 1], scale=norm.inverse[:, t:t + 1]
                                   ).then_inc(normalised, 1)

            def step(b, k, u, lagged):
                act.wait_ge(turned_rows[k], u + 1)
                if not isinstance(b, int) or b >= 2:
                    act.wait_ge(product_ready, b - 1)
                act.copy(rowsT[:, k], turned[:, 0:BATCH, :]).then_inc(rowsT_ready, 1)
                lagged(normalise)
            over_batches(act, s, step)
            normalise(*last_batch(s))

        @block.vector
        def _(dve):
            def finish(b, k, u):
                batch = bass.ds(b * (BATCH * D), BATCH * D)
                dve.wait_ge(normalised, (b + 1) * BATCH)
                dve.tensor_tensor(normal[:, k], normal[:, k], mem.gamma[:].unsqueeze(1).to_broadcast([P, BATCH, D]),
                                  ALU.mult).then_inc(weighed, 1)
                flat = normal[:, k].rearrange("p t d -> p (t d)")
                dve.wait_ge(weighed, b + 1)
                dve.sem_inc(passed, 1)
                dve.tensor_tensor(flat, flat, mem.h_beta[:, batch], ALU.add).then_inc(summed, 1)
                dve.wait_ge(summed, b + 1)
                reach(dve, stored[k], u * 16)
                dve.sem_inc(passed, 1)
                dve.scalar_tensor_tensor(result[:, k].rearrange("p t d -> p (t d)"), flat, 0.0, mem.x[:, batch],
                                         ALU.max, ALU.add).then_inc(finished, 1)

            def step(b, k, u, lagged):
                dve.wait_ge(own_landed[k], (u + 1) * 16)
                dve.wait_ge(product_ready, b + 1)
                dve.sem_inc(passed, 1)
                for t in range(BATCH):
                    dve.scalar_tensor_tensor(update[:, k, t, :], product[k][:, t, :],
                                             mem.scale[1][:, bass.ds(b * BATCH + t, 1)], own[:, k, t, :],
                                             ALU.mult, ALU.add).then_inc(combined, 1)
                dve.wait_ge(combined, (b + 1) * BATCH)
                measure_rows(norm, dve, b, lambda t: update[:, k, t, :])
                lagged(finish)
                make_scale_and_shift(norm, dve, b)
            over_batches(dve, s, step)
            finish(*last_batch(s))

        @block.sync
        def _(sp):
            def store(b, k, u):
                sp.wait_ge(finished, b + 1)
                sp.dma_start(node_rows(out, b), result[:, k]).then_inc(stored[k], 16)

            def step(b, k, u, lagged):
                if not isinstance(b, int) or b >= 2:
                    sp.wait_ge(combined, (b - 1) * BATCH)
                sp.dma_start(own[:, k].rearrange("p t d -> p (t d)"), mem.own_dram[bass.ds(b * P, P), :]
                             ).then_inc(own_landed[k], 16)
                if not isinstance(b, int) or b >= 2:
                    store(b - 2, k, u - 1)
            over_batches(sp, s, step)
            store(batches - 2, 0, batches // 2 - 1)
            first, full = (batches - 1) * BATCH * P, s.nodes // P - (batches - 1) * BATCH
            sp.wait_ge(finished, batches)
            sp.dma_start(out[first:first + full * P, :].rearrange("(t p) d -> p t d", p=P), result[:, 1, 0:full, :]
                         ).then_inc(stored[1], 16)
            sp.dma_start(out[first + full * P:s.nodes, :], result[0:s.nodes % P, 1, full, :]).then_inc(stored[1], 16)
            sp.wait_ge(stored[0], batches // 2 * 16)
            sp.wait_ge(stored[1], (batches // 2 + 1) * 16)




def gnn_kernel(nc, x, src, dst, edge_attr, fc_w, fc_b, w_layer0, w_msg, b_msg, w_upd, b_upd, gamma, beta, out):
    nodes, d = x.shape
    s = Shapes(nodes, src.shape[0], d, fc_w.shape[1])
    mem = Memory()
    with ExitStack() as ctx:
        def sb(name, shape, dt=F32):
            return ctx.enter_context(nc.sbuf_tensor(name, shape, dt))

        rows = s.tiles * P
        mem.x_dram = x
        mem.z_dram = nc.dram_tensor("z_dram", (rows, s.hid), F32).ap()
        mem.own_dram = nc.dram_tensor("own_dram", (s.tiles // BATCH * P, BATCH * P), F32).ap()
        mem.message_dram = nc.dram_tensor("message_dram", (rows, d), F32).ap()
        mem.result_dram = nc.dram_tensor("result_dram", (s.rows * ROW, d), F32).ap()
        mem.reset_dram = nc.dram_tensor("reset_dram", (s.rows * CH, GROUP), BF16).ap()
        mem.segment_dram = [nc.dram_tensor(f"segment_dram{n}", (s.rows * CH, GROUP), F32).ap() for n in range(2)]
        mem.x = sb("x", [P, s.tiles * d])
        mem.ident_wide = sb("ident_wide", [P, 2 * P])
        mem.ident = mem.ident_wide[:, 1:1 + P]
        mem.ident_bf = sb("ident_bf", [P, P], BF16)
        mem.ones = sb("ones", [P, P])
        mem.eps = sb("eps", [P, 1])
        mem.node_number = sb("node_number", [P, s.tiles])
        mem.row_number = sb("row_number", [P, P], I32)
        mem.partition_number = sb("partition_number", [P, 1], I32)
        mem.index = [sb(f"index{n}", [P, ROW], I32) for n in range(2)]
        mem.resets = [sb(f"resets{n}", [P, ROW], BF16) for n in range(2)]
        mem.heads = [sb(f"heads{n}", [P, s.rows * CH]) for n in range(2)]
        mem.twice_group = [sb(f"twice_group{n}", [P, s.tiles]) for n in range(2)]
        mem.row_balance = [sb(f"row_balance{n}", [P, s.tiles]) for n in range(2)]
        mem.ends = [sb(f"ends{n}", [P, 1 + s.tiles]) for n in range(2)]
        mem.last = [sb(f"last{n}", [P, s.tiles], I32) for n in range(2)]
        mem.scale = [sb(f"scale{n}", [P, s.tiles]) for n in range(2)]
        mem.inverse_root = sb("inverse_root", [P, s.tiles])
        mem.shift = sb("shift", [P, s.tiles])
        mem.node_half = sb("node_half", [P, s.tiles])
        mem.fc_w = sb("fc_w", [P, s.hid])
        mem.fc_b = sb("fc_b", [P, s.chunks])
        mem.w_own = sb("w_own", [P, d])
        mem.w_agg = sb("w_agg", [P, s.chunks, d])
        mem.wm_own = sb("wm_own", [P, d])
        mem.wm_attr = sb("wm_attr", [P, d])
        mem.b_msg = sb("b_msg", [P, 1])
        mem.wu_own = sb("wu_own", [P, d])
        mem.wu_mean = sb("wu_mean", [P, d])
        mem.b_upd = sb("b_upd", [P, d])
        mem.gamma = sb("gamma", [P, d])
        mem.beta = sb("beta", [P, d])
        ctx.enter_context(nc.allow_non_contiguous_dma(reason="biases onto partitions, once"))
        mem.weights = [
            (mem.fc_w[:], fc_w),
            (mem.fc_b[:], fc_b.rearrange("(c p) -> p c", p=P)),
            (mem.w_own[:], w_layer0[0:d, :]),
            (mem.w_agg[:], w_layer0[d:, :].rearrange("(c p) n -> p c n", p=P)),
            (mem.wm_own[:], w_msg[0:d, :]),
            (mem.wm_attr[:], w_msg[d:, :]),
            (mem.b_msg[:], b_msg.rearrange("(p a) -> p a", a=1)),
            (mem.wu_own[:], w_upd[0:d, :]),
            (mem.wu_mean[:], w_upd[d:, :]),
            (mem.b_upd[:], b_upd.rearrange("(a d) -> a d", a=1).to_broadcast([P, d])),
            (mem.gamma[:], gamma.rearrange("(a d) -> a d", a=1).to_broadcast([P, d])),
            (mem.beta[:], beta.rearrange("(a d) -> a d", a=1).to_broadcast([P, d])),
        ]
        mem.weights_landed = nc.alloc_semaphore("weights_landed")
        with ExitStack() as early:
            def rows_of(name, dt=F32):
                return early.enter_context(nc.sbuf_tensor(name, [P, ROW], dt))

            mem.src_rows, mem.dst_rows = rows_of("src_rows", I32), rows_of("dst_rows", I32)
            mem.key_a, mem.key_b = rows_of("key_a"), rows_of("key_b")
            mem.sorted_keys = mem.key_b
            with ExitStack() as given:
                mem.src_given, mem.dst_given = (
                    given.enter_context(nc.sbuf_tensor(f"{x}_given", [P, ROW], F32)) for x in ("src", "dst"))
                setup(nc, s, mem, src, dst)
                make_tables(nc, s, mem, 1, mem.dst_given, mem.src_given, mem.index[1], mem.resets[1], "keep")
            sort_and_first_nodes(nc, s, mem)
            nc.clear_and_free_semaphores([mem.weights_landed])
            nc.all_engine_barrier()
            mem.src_sorted, mem.dst_sorted = rows_of("src_sorted"), rows_of("dst_sorted")
            unpack_sorted_keys(nc, s, mem)
            make_tables(nc, s, mem, 0, mem.src_sorted, mem.dst_sorted, mem.index[0], mem.resets[0], "reset")
        edges_of_layer0(nc, s, mem)
        find_ends(nc, s, mem, 0)
        mem.h_beta = sb("h_beta", [P, s.tiles * d])
        nodes_between_layers(nc, s, mem)
        find_ends(nc, s, mem, 1)
        edges_of_layer1(nc, s, mem, edge_attr)
        nodes_after_layer1(nc, s, mem, out)


_INS = ["x", "src", "dst", "edge_attr_128", "L0_gnn_fc_w", "L0_gnn_fc_b", "L0_gnn_weights_matrix", "L1_gnn_W_msg",
        "L1_gnn_b_msg", "L1_gnn_W_upd", "L1_gnn_b_upd", "L1_gnn_gamma", "L1_gnn_beta"]


def kernel(**inputs):
    import numpy as _np
    import concourse.bacc as _bacc
    from concourse import mybir as _mybir
    from concourse.bass_utils import run_bass_kernel_spmd as _run

    nc = _bacc.Bacc("TRN2", target_bir_lowering=False, num_devices=1)
    arrays, args = {}, []
    for name in _INS:
        a = _np.ascontiguousarray(inputs[name])
        arrays[f"in_{name}_dram"] = a
        args.append(nc.dram_tensor(f"in_{name}_dram", a.shape, _mybir.dt.from_np(a.dtype), kind="ExternalInput").ap())
    x = inputs["x"]
    out = nc.dram_tensor("out_0_dram", tuple(x.shape), _mybir.dt.from_np(_np.dtype("float32")),
                         kind="ExternalOutput").ap()
    gnn_kernel(nc, *args, out)
    r = _run(nc, [arrays], core_ids=[0])
    return r.results[0]["out_0_dram"]
```
